# Optimizing a Trainium2 kernel written in Bass

```python
import numpy as np
import jax
import jax.numpy as jnp

def _softmax(x, axis=-1):
    return jax.nn.softmax(x, axis=axis)

def _gelu(x):
    return jax.nn.gelu(x, approximate=True)

def _silu(x):
    return jax.nn.silu(x)

def _sigmoid(x):
    return jax.nn.sigmoid(x)

def _layernorm(x, axis=-1, eps=1e-05):
    m = jnp.mean(x, axis=axis, keepdims=True)
    v = jnp.var(x, axis=axis, keepdims=True)
    return (x - m) / jnp.sqrt(v + eps)

def _scatter_add(tgt, idx, src, axis=0):
    return tgt.at[idx].add(src)

def _segment_sum(src, seg, n):
    return jax.ops.segment_sum(src, seg, n)
kernel_name = 'mk_adaln_d1_jaxref_r8_839fc0'

def setup_inputs(seed: int=0):
    np.random.seed(seed)
    _w = jnp.asarray

    def _L0_attn_setup():
        import jax, jax.numpy as jnp
        import numpy as np
        DIM = 128
        EXPAND = 2
        D_INNER = DIM * EXPAND
        D_STATE = 16
        D_CONV = 4
        DT_RANK = max(16, DIM // 16)
        BATCH = 2
        SEQ = 128
        EPS_RMS = 1e-06

        def _ssm_forward(x, W_in, W_conv, b_conv, W_x, W_dt, b_dt, A_log, D, rms_w, W_out):
            b, s, _ = x.shape
            xz = jnp.einsum('bsd,ed->bse', x, W_in)
            x_in, z = jnp.split(xz, 2, axis=-1)
            xpad = jnp.pad(x_in, ((0, 0), (D_CONV - 1, 0), (0, 0)))
            xc = b_conv
            for k in range(D_CONV):
                xc = xc + W_conv[:, k] * xpad[:, k:k + s, :]
            xc = jax.nn.silu(xc)
            dbl = jnp.einsum('bsd,ed->bse', xc, W_x)
            dt, Bm, Cm = jnp.split(dbl, [DT_RANK, DT_RANK + D_STATE], axis=-1)
            dt = jax.nn.softplus(jnp.einsum('bsr,dr->bsd', dt, W_dt) + b_dt) + 0.0001
            A = -jnp.exp(A_log)
            dA = jnp.exp(jnp.clip(dt[..., None] * A, -10.0, 10.0))
            dBu = dt[..., None] * Bm[:, :, None, :] * xc[..., None]

            def step(h, inp):
                dA_t, dBu_t, C_t = inp
                h = dA_t * h + dBu_t
                y = jnp.einsum('bdn,bn->bd', h, C_t)
                return (h, y)
            h0 = jnp.zeros((b, D_INNER, D_STATE), x.dtype)
            _, ys = jax.lax.scan(step, h0, (jnp.moveaxis(dA, 1, 0), jnp.moveaxis(dBu, 1, 0), jnp.moveaxis(Cm, 1, 0)))
            y = jnp.moveaxis(ys, 0, 1) + xc * D
            y = y * jax.nn.silu(z)
            y = y * jax.lax.rsqrt(jnp.mean(y * y, axis=-1, keepdims=True) + EPS_RMS) * rms_w
            return jnp.einsum('bse,de->bsd', y, W_out)
        key = jax.random.key(seed)
        ks = jax.random.split(key, 10)

        def nrm(k, shape, scale=0.02):
            return jax.random.normal(k, shape, jnp.float32) * scale
        x = jax.random.normal(ks[0], (BATCH, SEQ, DIM), jnp.float32)
        W_in = nrm(ks[1], (2 * D_INNER, DIM))
        W_conv = nrm(ks[2], (D_INNER, D_CONV), 0.1)
        b_conv = nrm(ks[3], (D_INNER,), 0.01)
        W_x = nrm(ks[4], (DT_RANK + 2 * D_STATE, D_INNER))
        dt_std = DT_RANK ** (-0.5) * 0.1
        W_dt = jax.random.uniform(ks[5], (D_INNER, DT_RANK), jnp.float32, -dt_std, dt_std)
        b_dt = jax.random.uniform(ks[6], (D_INNER,), jnp.float32, 0.001, 0.1)
        A = jnp.arange(1, D_STATE + 1, dtype=jnp.float32)[None, :] + 0.01 * jax.random.normal(ks[7], (D_INNER, D_STATE), jnp.float32)
        A_log = jnp.log(A + 1e-08)
        D = jnp.ones((D_INNER,), jnp.float32) * 0.1
        rms_w = jnp.ones((D_INNER,), jnp.float32)
        W_out = nrm(ks[8], (DIM, D_INNER))
        return dict(x=x, W_in=W_in, W_conv=W_conv, b_conv=b_conv, W_x=W_x, W_dt=W_dt, b_dt=b_dt, A_log=A_log, D=D, rms_w=rms_w, W_out=W_out)
    _L0_attn_in = _L0_attn_setup()

    def _L0_ffn_setup():
        import jax, jax.numpy as jnp
        import numpy as np
        B, N, D, H, E = (4, 128, 128, 16, 8)
        DK = D // H
        HID = 4 * D
        EPS = 1e-05

        def _layernorm(x, w, b):
            m = jnp.mean(x, axis=-1, keepdims=True)
            v = jnp.mean(jnp.square(x - m), axis=-1, keepdims=True)
            return (x - m) * jax.lax.rsqrt(v + EPS) * w + b

        def _msa(x, w_qkv, w_proj):
            b, n, d = x.shape
            qkv = (x @ w_qkv).reshape(b, n, 3, H, DK)
            q = qkv[:, :, 0].transpose(0, 2, 1, 3)
            k = qkv[:, :, 1].transpose(0, 2, 1, 3)
            v = qkv[:, :, 2].transpose(0, 2, 1, 3)
            attn = jnp.einsum('bhnd,bhmd->bhnm', q, k) * (1.0 / np.sqrt(DK))
            attn = jax.nn.softmax(attn, axis=-1)
            y = jnp.einsum('bhnm,bhmd->bhnd', attn, v)
            y = y.transpose(0, 2, 1, 3).reshape(b, n, d)
            return y @ w_proj

        def _moe_mlp(x, gate_w, gate_b, w1, w2):
            b, n, d = x.shape
            xf = x.reshape(b * n, d)
            logits = xf @ gate_w + gate_b
            one_hot = jax.nn.one_hot(jnp.argmax(logits, axis=-1), E, dtype=xf.dtype)
            h = jax.nn.gelu(jnp.einsum('td,edh->teh', xf, w1), approximate=True)
            y = jnp.einsum('teh,ehd->ted', h, w2)
            out = jnp.einsum('te,ted->td', one_hot, y)
            return out.reshape(b, n, d)
        key = jax.random.key(seed)
        ks = jax.random.split(key, 8)
        s = 0.02
        return {'x': jax.random.normal(ks[0], (B, N, D), jnp.float32), 'ln1_w': jnp.ones((D,), jnp.float32), 'ln1_b': jnp.zeros((D,), jnp.float32), 'w_qkv': jax.random.normal(ks[1], (D, 3 * D), jnp.float32) * s, 'w_proj': jax.random.normal(ks[2], (D, D), jnp.float32) * s, 'ln2_w': jnp.ones((D,), jnp.float32), 'ln2_b': jnp.zeros((D,), jnp.float32), 'gate_w': jax.random.normal(ks[3], (D, E), jnp.float32) * s, 'gate_b': jnp.zeros((E,), jnp.float32), 'w1': jax.random.normal(ks[4], (E, D, HID), jnp.float32) * s, 'w2': jax.random.normal(ks[5], (E, HID, D), jnp.float32) * s}
    _L0_ffn_in = _L0_ffn_setup()
    _L0_c = _w((lambda *s: np.random.randn(*s).astype(np.float32) * 0.05)(16, 128))
    _L0_wmod = _w((lambda *s: np.random.randn(*s).astype(np.float32) * 0.05)(128, 6 * 128) * 128 ** (-0.5))
    _d = {'L0_attn_x': _L0_attn_in['x'], 'L0_attn_W_in': _L0_attn_in['W_in'], 'L0_attn_W_conv': _L0_attn_in['W_conv'], 'L0_attn_b_conv': _L0_attn_in['b_conv'], 'L0_attn_W_x': _L0_attn_in['W_x'], 'L0_attn_W_dt': _L0_attn_in['W_dt'], 'L0_attn_b_dt': _L0_attn_in['b_dt'], 'L0_attn_A_log': _L0_attn_in['A_log'], 'L0_attn_D': _L0_attn_in['D'], 'L0_attn_rms_w': _L0_attn_in['rms_w'], 'L0_attn_W_out': _L0_attn_in['W_out'], 'L0_ffn_ln1_w': _L0_ffn_in['ln1_w'], 'L0_ffn_ln1_b': _L0_ffn_in['ln1_b'], 'L0_ffn_w_qkv': _L0_ffn_in['w_qkv'], 'L0_ffn_w_proj': _L0_ffn_in['w_proj'], 'L0_ffn_ln2_w': _L0_ffn_in['ln2_w'], 'L0_ffn_ln2_b': _L0_ffn_in['ln2_b'], 'L0_ffn_gate_w': _L0_ffn_in['gate_w'], 'L0_ffn_gate_b': _L0_ffn_in['gate_b'], 'L0_ffn_w1': _L0_ffn_in['w1'], 'L0_ffn_w2': _L0_ffn_in['w2'], 'L0_c': _L0_c, 'L0_wmod': _L0_wmod}
    _x0 = _d['L0_attn_x']
    _d['L0_attn_x'] = jax.random.normal(jax.random.fold_in(jax.random.key(seed), 1), (16, 256, 128), dtype=_x0.dtype)
    del _x0
    return _d

def reference(L0_attn_x, L0_attn_W_in, L0_attn_W_conv, L0_attn_b_conv, L0_attn_W_x, L0_attn_W_dt, L0_attn_b_dt, L0_attn_A_log, L0_attn_D, L0_attn_rms_w, L0_attn_W_out, L0_ffn_ln1_w, L0_ffn_ln1_b, L0_ffn_w_qkv, L0_ffn_w_proj, L0_ffn_ln2_w, L0_ffn_ln2_b, L0_ffn_gate_w, L0_ffn_gate_b, L0_ffn_w1, L0_ffn_w2, L0_c, L0_wmod):

    def _L0_attn_ref(x, W_in, W_conv, b_conv, W_x, W_dt, b_dt, A_log, D, rms_w, W_out):
        import jax, jax.numpy as jnp
        import numpy as np
        DIM = 128
        EXPAND = 2
        D_INNER = DIM * EXPAND
        D_STATE = 16
        D_CONV = 4
        DT_RANK = max(16, DIM // 16)
        BATCH = 2
        SEQ = 128
        EPS_RMS = 1e-06

        def _ssm_forward(x, W_in, W_conv, b_conv, W_x, W_dt, b_dt, A_log, D, rms_w, W_out):
            b, s, _ = x.shape
            xz = jnp.einsum('bsd,ed->bse', x, W_in)
            x_in, z = jnp.split(xz, 2, axis=-1)
            xpad = jnp.pad(x_in, ((0, 0), (D_CONV - 1, 0), (0, 0)))
            xc = b_conv
            for k in range(D_CONV):
                xc = xc + W_conv[:, k] * xpad[:, k:k + s, :]
            xc = jax.nn.silu(xc)
            dbl = jnp.einsum('bsd,ed->bse', xc, W_x)
            dt, Bm, Cm = jnp.split(dbl, [DT_RANK, DT_RANK + D_STATE], axis=-1)
            dt = jax.nn.softplus(jnp.einsum('bsr,dr->bsd', dt, W_dt) + b_dt) + 0.0001
            A = -jnp.exp(A_log)
            dA = jnp.exp(jnp.clip(dt[..., None] * A, -10.0, 10.0))
            dBu = dt[..., None] * Bm[:, :, None, :] * xc[..., None]

            def step(h, inp):
                dA_t, dBu_t, C_t = inp
                h = dA_t * h + dBu_t
                y = jnp.einsum('bdn,bn->bd', h, C_t)
                return (h, y)
            h0 = jnp.zeros((b, D_INNER, D_STATE), x.dtype)
            _, ys = jax.lax.scan(step, h0, (jnp.moveaxis(dA, 1, 0), jnp.moveaxis(dBu, 1, 0), jnp.moveaxis(Cm, 1, 0)))
            y = jnp.moveaxis(ys, 0, 1) + xc * D
            y = y * jax.nn.silu(z)
            y = y * jax.lax.rsqrt(jnp.mean(y * y, axis=-1, keepdims=True) + EPS_RMS) * rms_w
            return jnp.einsum('bse,de->bsd', y, W_out)
        return _ssm_forward(x, W_in, W_conv, b_conv, W_x, W_dt, b_dt, A_log, D, rms_w, W_out)

    def _L0_ffn_ref(x, ln1_w, ln1_b, w_qkv, w_proj, ln2_w, ln2_b, gate_w, gate_b, w1, w2):
        import jax, jax.numpy as jnp
        import numpy as np
        B, N, D, H, E = (4, 128, 128, 16, 8)
        DK = D // H
        HID = 4 * D
        EPS = 1e-05

        def _layernorm(x, w, b):
            m = jnp.mean(x, axis=-1, keepdims=True)
            v = jnp.mean(jnp.square(x - m), axis=-1, keepdims=True)
            return (x - m) * jax.lax.rsqrt(v + EPS) * w + b

        def _msa(x, w_qkv, w_proj):
            b, n, d = x.shape
            qkv = (x @ w_qkv).reshape(b, n, 3, H, DK)
            q = qkv[:, :, 0].transpose(0, 2, 1, 3)
            k = qkv[:, :, 1].transpose(0, 2, 1, 3)
            v = qkv[:, :, 2].transpose(0, 2, 1, 3)
            attn = jnp.einsum('bhnd,bhmd->bhnm', q, k) * (1.0 / np.sqrt(DK))
            attn = jax.nn.softmax(attn, axis=-1)
            y = jnp.einsum('bhnm,bhmd->bhnd', attn, v)
            y = y.transpose(0, 2, 1, 3).reshape(b, n, d)
            return y @ w_proj

        def _moe_mlp(x, gate_w, gate_b, w1, w2):
            b, n, d = x.shape
            xf = x.reshape(b * n, d)
            logits = xf @ gate_w + gate_b
            one_hot = jax.nn.one_hot(jnp.argmax(logits, axis=-1), E, dtype=xf.dtype)
            h = jax.nn.gelu(jnp.einsum('td,edh->teh', xf, w1), approximate=True)
            y = jnp.einsum('teh,ehd->ted', h, w2)
            out = jnp.einsum('te,ted->td', one_hot, y)
            return out.reshape(b, n, d)
        x = x + _msa(_layernorm(x, ln1_w, ln1_b), w_qkv, w_proj)
        x = x + _moe_mlp(_layernorm(x, ln2_w, ln2_b), gate_w, gate_b, w1, w2)
        return x
    x = L0_attn_x
    mod = (_silu(L0_c) @ L0_wmod).reshape(L0_c.shape[0], 6, 1, -1)
    sa, ca, ga, sb, cb, gb = (mod[:, 0], mod[:, 1], mod[:, 2], mod[:, 3], mod[:, 4], mod[:, 5])
    ga = (2 * (ga >= 0) - 1) * jnp.maximum(jnp.abs(ga), 0.25)
    gb = (2 * (gb >= 0) - 1) * jnp.maximum(jnp.abs(gb), 0.25)
    h = _layernorm(x, axis=-1) * (1 + ca) + sa
    x = x + ga * _L0_attn_ref(h, L0_attn_W_in, L0_attn_W_conv, L0_attn_b_conv, L0_attn_W_x, L0_attn_W_dt, L0_attn_b_dt, L0_attn_A_log, L0_attn_D, L0_attn_rms_w, L0_attn_W_out)
    h = _layernorm(x, axis=-1) * (1 + cb) + sb
    x = x + gb * _L0_ffn_ref(h, L0_ffn_ln1_w, L0_ffn_ln1_b, L0_ffn_w_qkv, L0_ffn_w_proj, L0_ffn_ln2_w, L0_ffn_ln2_b, L0_ffn_gate_w, L0_ffn_gate_b, L0_ffn_w1, L0_ffn_w2)
    return x

_drawn_inputs = setup_inputs


def setup_inputs(seed=0):
    import zlib

    import numpy as np

    out = dict(_drawn_inputs(seed))
    spreads = {'L0_attn_D': (0.10000000149011612, 0.6),
     'L0_attn_rms_w': (1.0, 0.6),
     'L0_ffn_ln1_w': (1.0, 0.6),
     'L0_ffn_ln1_b': (0.0, 0.8),
     'L0_ffn_ln2_w': (1.0, 0.6),
     'L0_ffn_ln2_b': (0.0, 0.8),
     'L0_ffn_gate_b': (0.0, 0.69)}
    factors = {'L0_attn_b_conv': 8.0,
     'L0_attn_W_x': 8.0,
     'L0_attn_W_dt': 8.0,
     'L0_attn_b_dt': 8.0,
     'L0_attn_A_log': 8.0,
     'L0_ffn_w_qkv': 8.0,
     'L0_ffn_w_proj': 8.0,
     'L0_ffn_gate_w': 4.646,
     'L0_ffn_w1': 4.182,
     'L0_ffn_w2': 4.112}
    for name, (base, spread) in spreads.items():
        noise = np.random.default_rng([zlib.crc32(name.encode()), seed]).standard_normal(out[name].shape)
        drawn = base * np.exp(spread * noise) if base else spread * noise
        out[name] = jnp.asarray(drawn.astype(out[name].dtype))
    for name, factor in factors.items():
        out[name] = (out[name] * factor).astype(out[name].dtype)
    return out
```

```python
import concourse.bass as bass
from concourse import mybir
from contextlib import ExitStack


def adaln_block(nc, io, out):
    fp32 = mybir.dt.float32
    bf16 = mybir.dt.bfloat16
    ALU = mybir.AluOpType
    ACT = mybir.ActivationFunctionType
    AX = mybir.AxisListType

    B, D, T = io["x"].shape
    P = 128
    NH = io["w_inT"].shape[1] // P // 2
    NS = io["a_log"].shape[2]
    TAPS = io["w_conv"].shape[2]
    R = io["w_dtT"].shape[0]
    DK = 8
    NG = D // DK // 4
    E = io["gate_w"].shape[1]
    HC = io["w1"].shape[2] // P
    NC = T // P
    U = 4
    NU = NS // U
    ZU = NH * U
    FILLS = NC * (NG // 2) * 4
    LEAST = -43.0
    RD = 4
    assert D == P and NC * P == T and FILLS == NG * 4 and NS % U == 0 and U == 4

    ctx = ExitStack()
    with ctx:
        def sb(name, shape, dt=fp32):
            return ctx.enter_context(nc.sbuf_tensor(name, shape, dt))

        per = {}
        S = {}

        def event(name, times=1):
            S[name] = ctx.enter_context(nc.semaphore(name))
            per[name] = times

        w_inT = sb("w_inT", [P, 2 * NH * P])
        w_conv = sb("w_conv", [P, NH, TAPS])
        b_conv = sb("b_conv", [P, NH])
        w_dbl = sb("w_dbl", [P, NH, 3 * 2 * NS])
        w_rank = sb("w_rank", [P, NH, R])
        w_dtT = sb("w_dtT", [R, NH * P])
        b_dt = sb("b_dt", [P, NH])
        a_neg = sb("a_neg", [P, NH, NS])
        a_log = sb("a_log", [P, NH, NS])
        skip = sb("skip", [P, NH])
        rms_w = sb("rms_w", [P, NH])
        w_outT = sb("w_outT", [P, NH, D])
        ln = sb("ln", [P, 4])
        w_q = sb("w_q", [P, NG, P])
        w_k = sb("w_k", [P, NG, P])
        w_v = sb("w_v", [P, D])
        w_proj = sb("w_proj", [P, NG, D])
        gate_w = sb("gate_w", [P, E])
        gate_b = sb("gate_b", [1, E])
        w1 = sb("w1", [P, E, HC * P])
        w2 = sb("w2", [P, E, HC, D])
        cT = sb("cT", [P, B])
        w_mod = sb("w_mod", [P, 6, P])
        c_tmp = sb("c_tmp", [P, 3, B])
        mods = sb("mods", [P, 6, B])
        mods_abs = sb("mods_abs", [P, 2, B])
        ident = sb("ident", [P, P])
        ident_b = sb("ident_b", [P, P], bf16)
        mean_d = sb("mean_d", [P, P])
        mean_i = sb("mean_i", [P, P])
        pick = sb("pick", [96, 2 * NS, P], bf16)
        spread = sb("spread", [P, P])
        ones_row = sb("ones_row", [1, P])
        eps_ln = sb("eps_ln", [P, 1])
        eps_rms = sb("eps_rms", [P, 1])
        one = sb("one", [P, 1])
        zero = sb("zero", [P, 1])
        zeros = sb("zeros", [P, ZU, 1])
        k_bias = sb("k_bias", [P, 1])
        rank_e = sb("rank_e", [P, E])

        x_all = sb("x_all", [P, B, T])
        xf_all = sb("xf_all", [P, B, T])

        x_cur = sb("x_cur", [P, T])
        mod = sb("mod", [P, 6])
        cen = sb("cen", [P, T])
        sq = sb("sq", [P, NH, T])
        lnv = sb("lnv", [P, T])
        rs = sb("rs", [P, T])
        h1 = sb("h1", [P, T])
        xp = sb("xp", [P, NH, TAPS - 1 + T])
        pz = sb("pz", [P, 2 * NH, T])
        pm = sb("pm", [P, 2 * NH, T])
        sil = sb("sil", [P, 2 * NH, T])
        rank_s = sb("rank_s", [R, T])
        bc_v = sb("bc_v", [96, T])
        bc_r = sb("bc_r", [96, T])
        bc = sb("bc", [96, T], bf16)
        sp_a = sb("sp_a", [P, NH, T])
        sp_r = sb("sp_r", [P, NH, T])
        dt_s = sb("dt_s", [P, NH, T])
        u_s = sb("u_s", [P, NH, T])
        dA = [sb(f"dA{k}", [P, ZU, T]) for k in range(2)]
        H = [sb(f"H{k}", [P, ZU, T]) for k in range(2)]
        y_s = sb("y_s", [P, NH, T])
        x1 = sb("x1", [P, T])
        h2 = sb("h2", [P, T])

        acen = sb("acen", [P, T])
        asq = sb("asq", [P, T])
        alnv = sb("alnv", [P, T])
        ars = sb("ars", [P, T])
        hn = sb("hn", [P, T])
        qP = sb("qP", [P, NG, T])
        kP = sb("kP", [P, NG, T])
        vA = sb("vA", [P, NC, NG * 4, 32])
        mxp = sb("mxp", [P, NC, NG, P])
        PT = sb("PT", [P, RD, NC, T])
        yh = sb("yh", [P, NG, T])
        rinv = sb("rinv", [P, NG, T])
        x2 = sb("x2", [P, T])

        def bank(k):
            return ctx.enter_context(nc.psum_tensor(f"bank{k}", [P, 512], fp32))

        mixb, ring0, ring1, ybank, ab, vb, s0, s1 = [bank(k) for k in range(8)]
        ring = [ring0, ring1]
        sbank = [s0, s1]
        av = [ab, vb]

        s_load = ctx.enter_context(nc.semaphore("s_load"))
        s_const = ctx.enter_context(nc.semaphore("s_const"))
        s_mod = ctx.enter_context(nc.semaphore("s_mod"))
        s_silc = ctx.enter_context(nc.semaphore("s_silc"))
        s_setup = ctx.enter_context(nc.semaphore("s_setup"))
        s_chain = ctx.enter_context(nc.semaphore("s_chain"))

        loads = [(x_all, io["x"].rearrange("b d t -> d b t")), (w_inT, io["w_inT"]), (w_conv, io["w_conv"]),
                 (b_conv, io["b_conv"]), (w_dbl, io["w_dbl"]), (w_rank, io["w_rank"]), (w_dtT, io["w_dtT"]),
                 (b_dt, io["b_dt"]), (a_log, io["a_log"]), (skip, io["skip"]), (rms_w, io["rms_w"]),
                 (w_outT, io["w_outT"]), (ln, io["ln"]), (w_q, io["w_q"]), (w_k, io["w_k"]), (w_v, io["w_v"]),
                 (w_proj, io["w_proj"]), (gate_w, io["gate_w"]), (gate_b, io["gate_b"]), (cT, io["cT"]),
                 (w_mod, io["w_mod"]), (w1, io["w1"].rearrange("e d h -> d e h")),
                 (w2, io["w2"].rearrange("e (c p) d -> p e c d", p=P))]

        with nc.Block() as block:
            @block.sync
            def _(sp):
                for tile, src in loads:
                    sp.dma_start(tile[:], src).then_inc(s_load, 16)
                sp.wait_ge(s_load, 16 * len(loads))

            @block.gpsimd
            def _(pool):
                nc.gpsimd.memset(ident[:], 0.0)
                nc.gpsimd.memset(mean_d[:], 1.0 / D)
                nc.gpsimd.memset(mean_i[:], 1.0 / (NH * P))
                nc.gpsimd.memset(pick[:], 0.0)
                nc.gpsimd.memset(spread[:], 0.0)
                nc.gpsimd.memset(ones_row[:], 1.0)
                nc.gpsimd.memset(eps_ln[:], 1e-5)
                nc.gpsimd.memset(eps_rms[:], 1e-6)
                nc.gpsimd.memset(one[:], 1.0)
                nc.gpsimd.memset(zero[:], 0.0)
                nc.gpsimd.memset(k_bias[:], 0.0).then_inc(s_const, 1)
                pool.wait_ge(s_const, 1)
                nc.gpsimd.affine_select(out=ident[:], in_=ident[:], compare_op=ALU.not_equal, fill=1.0, base=0,
                                        pattern=[[-1, P]], channel_multiplier=1)
                count = 1
                for part in range(3):
                    nc.gpsimd.affine_select(out=pick[:], in_=pick[:], compare_op=ALU.not_equal, fill=1.0,
                                            base=-2 * NS * part, pattern=[[-1, 2 * NS], [0, P]],
                                            channel_multiplier=1).then_inc(s_const, 1)
                    count += 1
                    pool.wait_ge(s_const, count)
                sp_v = spread[:].rearrange("p (j r) -> p j r", r=32)
                nc.gpsimd.affine_select(out=sp_v, in_=sp_v, compare_op=ALU.not_equal, fill=1.0, base=-DK,
                                        pattern=[[-32, 4], [0, 32]], channel_multiplier=1)
                for j in range(4):
                    nc.gpsimd.affine_select(out=k_bias[:], in_=k_bias[:], compare_op=ALU.not_equal, fill=-1.0,
                                            base=-32 * j - DK, pattern=[[0, 1]],
                                            channel_multiplier=1).then_inc(s_const, 1)
                    count += 1
                    pool.wait_ge(s_const, count)
                nc.gpsimd.iota(rank_e[:], pattern=[[-1, E]], base=E, channel_multiplier=0,
                               allow_small_or_imprecise_dtypes=True)
                nc.gpsimd.tensor_copy(ident_b[:], ident[:]).then_inc(s_const, 1)
                assert count + 1 == 9

            @block.scalar
            def _(act):
                act.wait_ge(s_load, 16 * len(loads))
                act.wait_ge(s_const, 9)
                nc.scalar.activation(a_neg[:], a_log[:], ACT.Exp, bias=zero[:]).then_inc(s_silc, 1)
                act.wait_ge(s_mod, 1)
                nc.scalar.activation(c_tmp[:, 1], c_tmp[:, 0], ACT.Exp, bias=zero[:], scale=-1.0).then_inc(s_silc, 1)
                act.wait_ge(s_silc, 2)
                nc.scalar.activation(c_tmp[:, 2], c_tmp[:, 1], ACT.Ln, bias=one[:]).then_inc(s_silc, 1)
                act.wait_ge(s_silc, 3)
                nc.scalar.activation(c_tmp[:, 1], c_tmp[:, 2], ACT.Exp, bias=zero[:], scale=-1.0).then_inc(s_silc, 1)

            @block.vector
            def _(dve):
                count = 0

                def link(ins):
                    nonlocal count
                    count += 1
                    ins.then_inc(s_mod, 1)
                    dve.wait_ge(s_mod, count)

                dve.wait_ge(s_load, 16 * len(loads))
                link(nc.vector.tensor_scalar(c_tmp[:, 0], cT[:], LEAST, None, ALU.max))
                nc.vector.memset(xp[:, :, 0:TAPS - 1], 0.0)
                nc.vector.memset(mxp[:], 0.0)
                nc.vector.memset(vA[:, :, :, DK:DK + 1], 1.0)
                nc.vector.memset(vA[:, :, :, DK + 1:32], 0.0)
                nc.vector.memset(zeros[:], 0.0)
                dve.wait_ge(s_silc, 1)
                nc.vector.tensor_scalar(a_neg[:], a_neg[:], -1.0, None, ALU.mult)
                dve.wait_ge(s_silc, 4)
                link(nc.vector.tensor_tensor(c_tmp[:, 0], cT[:], c_tmp[:, 1], ALU.mult))
                dve.wait_ge(s_setup, 1)
                link(nc.vector.tensor_copy(mods[:], mixb[:, 0:6 * B].rearrange("p (m b) -> p m b", b=B)))
                for m in (1, 4):
                    nc.vector.tensor_scalar(mods[:, m], mods[:, m], 1.0, None, ALU.add)
                for k, m in enumerate((2, 5)):
                    link(nc.vector.tensor_scalar(c_tmp[:, 1], mods[:, m], -1.0, None, ALU.mult))
                    link(nc.vector.tensor_tensor(mods_abs[:, k], mods[:, m], c_tmp[:, 1], ALU.max))
                    link(nc.vector.tensor_scalar(mods_abs[:, k], mods_abs[:, k], 0.25, None, ALU.max))
                    link(nc.vector.tensor_scalar(c_tmp[:, 2], mods[:, m], 0.0, 2.0, ALU.is_ge, ALU.mult))
                    link(nc.vector.tensor_scalar(c_tmp[:, 2], c_tmp[:, 2], -1.0, None, ALU.add))
                    link(nc.vector.tensor_tensor(mods[:, m], c_tmp[:, 2], mods_abs[:, k], ALU.mult))

            @block.tensor
            def _(pe):
                pe.wait_ge(s_mod, 2)
                for m in range(6):
                    last = nc.tensor.matmul(mixb[:, m * B:(m + 1) * B], w_mod[:, m], c_tmp[:, 0],
                                            start=True, stop=True)
                last.then_inc(s_setup, 1)

        for tag in ("ln1", "rms", "ln2", "at", "mo"):
            for step in ("mean", "cen", "sq", "var", "rs", "xn"):
                event(f"{tag}_{step}")
        for name, times in (("cur", 1), ("h1", 1), ("xz_x", 1), ("xp", 1), ("xz_z", 1), ("z", 1), ("cut", 1),
                            ("sig", 1), ("silu", 1), ("dbl", 1), ("rank", 1), ("bc", 1), ("dtp", 1),
                            ("softp", 1), ("dt", 1), ("za", NU), ("dA", NU), ("Bb", 2 * NU), ("Bused", 2 * NU),
                            ("Cb", 2 * NU), ("hc", 2 * NU), ("scan", NU), ("ysum", NU),
                            ("yraw", 1), ("yout", 1), ("mix", 1), ("x1", 1), ("h2", 1),
                            ("hn", 1), ("q", 2), ("qc", 2), ("k", 2), ("kc", 2), ("v", 1), ("vc", 1),
                            ("smax", FILLS), ("mx", FILLS), ("mxT", 1), ("qm", 1), ("st", FILLS),
                            ("pt", FILLS), ("pv", 2), ("pvc", 2), ("den", 2), ("rinv", 1), ("yn", 1),
                            ("proj", 1), ("x2", 1), ("xf", 1), ("fin", 1),
                            ("chv", 60), ("cha", 30)):
            event(name, times)

        lg = sb("lg", [P, NC, E])
        key = sb("key", [P, NC, E])
        top = sb("top", [P, 2, NC])
        hot = sb("hot", [P, NC, E], bf16)
        xfc = H[0][:, 0]
        xm = dA[0]
        gel = [H[1][:, 2 * k:2 * k + 2] for k in range(4)]
        ot = [y_s[:, k] for k in range(2)]
        banks = [ring0, ring1, s0, s1]
        NP_ = E * HC // 2
        for name, times in (("m_x", 1), ("m_lg", 1), ("m_hot", 1), ("m_mask", E // 2), ("m_xm", E // 2),
                            ("m_up", NP_), ("m_gel", NP_), ("m_y", 1), ("m_out", 1), ("m_chv", 20)):
            event(name, times)
        s_store = ctx.enter_context(nc.semaphore("s_store"))

        def waits(eng, i):
            turns = {1: i}

            def wait(name, k=1):
                n = per[name]
                if n not in turns:
                    turns[n] = eng.snap(i * n)
                eng.wait_ge(S[name], turns[n] + (k + 1))
            return wait

        def chained(eng, wait, name):
            count = [0]

            def link(ins):
                count[0] += 1
                ins.then_inc(S[name], 1)
                wait(name, count[0])

            def close():
                while count[0] < per[name]:
                    n = per[name] - count[0]
                    count[0] += n
                    eng.sem_inc(S[name], n)
            return link, close

        def start_counts(sp):
            for name in per:
                sp.sem_inc(S[name], 1)
            sp.sem_inc(s_store, 16)

        with nc.Block() as block:
            @block.sync
            def _(sp):
                start_counts(sp)

        with nc.Block() as block:
            @block.gpsimd
            def _(pool):
                with pool.Fori(0, B) as i:
                    wait = waits(pool, i)
                    wait("fin", 0)
                    nc.gpsimd.tensor_copy(x_cur[:], x_all[:, bass.ds(i, 1), :].rearrange("p a t -> p (a t)"))
                    nc.gpsimd.tensor_copy(mod[:], mods[:, :, bass.ds(i, 1)].rearrange("p m a -> p (m a)")).then_inc(S["cur"], 1)
                    wait("dt")
                    for g in range(NU):
                        wait("scan", g - 1 if g >= 2 else 0)
                        nc.gpsimd.tensor_tensor(dA[g % 2][:, :, 0:1], zeros[:], zeros[:], ALU.add)
                        for j in range(NH):
                            for n in range(U):
                                last = nc.gpsimd.tensor_scalar(dA[g % 2][:, j * U + n, 1:T], dt_s[:, j, 1:T],
                                                               a_neg[:, j, g * U + n:g * U + n + 1], -10.0,
                                                               ALU.mult, ALU.max)
                        last.then_inc(S["za"], 1)

            @block.scalar
            def _(act):
                with act.Fori(0, B) as i:
                    wait = waits(act, i)
                    link, close = chained(act, wait, "cha")

                    def norm(tag, source, square, variance, log_var, eps, result):
                        wait(f"{tag}_cen")
                        nc.scalar.activation(square, source, ACT.Square, bias=zero[:]).then_inc(S[f"{tag}_sq"], 1)
                        wait(f"{tag}_var")
                        link(nc.scalar.activation(log_var, variance, ACT.Ln, bias=eps))
                        nc.scalar.activation(result, log_var, ACT.Exp, bias=zero[:], scale=-0.5).then_inc(S[f"{tag}_rs"], 1)

                    norm("ln1", cen[:], sq[:, 0], mixb[:, T:2 * T], lnv[:], eps_ln[:], rs[:])
                    wait("xz_x")
                    nc.scalar.activation(xp[:, :, TAPS - 1:], mixb[:].rearrange("p (j t) -> p j t", t=T), ACT.Copy).then_inc(S["xp"], 1)
                    wait("xz_z")
                    nc.scalar.activation(pz[:, NH:2 * NH], mixb[:].rearrange("p (j t) -> p j t", t=T), ACT.Copy).then_inc(S["z"], 1)
                    wait("cut")
                    link(nc.scalar.activation(pm[:], pm[:], ACT.Exp, bias=zero[:], scale=-1.0))
                    link(nc.scalar.activation(pm[:], pm[:], ACT.Ln, bias=one[:]))
                    nc.scalar.activation(pm[:], pm[:], ACT.Exp, bias=zero[:], scale=-1.0).then_inc(S["sig"], 1)
                    wait("dtp")
                    for j in range(NH):
                        last = nc.scalar.activation(sp_a[:, j], mixb[:, j * T:(j + 1) * T], ACT.Abs, bias=b_dt[:, j:j + 1])
                    link(last)
                    link(nc.scalar.activation(sp_a[:], sp_a[:], ACT.Exp, bias=zero[:], scale=-1.0))
                    nc.scalar.activation(sp_a[:], sp_a[:], ACT.Ln, bias=one[:]).then_inc(S["softp"], 1)
                    for g in range(NU):
                        wait("za", g + 1)
                        nc.scalar.activation(dA[g % 2][:, :, 1:T], dA[g % 2][:, :, 1:T], ACT.Exp,
                                             bias=zero[:]).then_inc(S["dA"], 1)
                    norm("rms", y_s[:], sq[:], mixb[:, T:2 * T], lnv[:], eps_rms[:], rs[:])
                    norm("ln2", cen[:], sq[:, 0], mixb[:, T:2 * T], lnv[:], eps_ln[:], rs[:])
                    norm("at", acen[:], asq[:], ab[:, T:2 * T], alnv[:], eps_ln[:], ars[:])
                    for half in range(2):
                        wait("q", half + 1)
                        nc.scalar.activation(qP[:, 2 * half:2 * half + 2], av[half][:].rearrange("p (g t) -> p g t", t=T), ACT.Copy).then_inc(S["qc"], 1)
                    for half in range(2):
                        wait("k", half + 1)
                        nc.scalar.activation(kP[:, 2 * half:2 * half + 2], av[half][:].rearrange("p (g t) -> p g t", t=T), ACT.Identity, bias=k_bias[:]).then_inc(S["kc"], 1)
                    for f in range(FILLS):
                        wait("st", f + 1)
                        nc.scalar.activation(PT[:, f % RD], sbank[f % 2][:].rearrange("p (c t) -> p c t", t=T), ACT.Exp,
                                             bias=zero[:], scale=float(DK) ** -0.5).then_inc(S["pt"], 1)
                        if f % 8 == 7:
                            half = f // 8
                            wait("pv", half + 1)
                            nc.scalar.activation(yh[:, 2 * half:2 * half + 2], av[half][:].rearrange("p (g t) -> p g t", t=T), ACT.Copy).then_inc(S["pvc"], 1)
                    for half in range(2):
                        wait("den", half + 1)
                        link(nc.scalar.activation(rinv[:, 2 * half:2 * half + 2], av[half][:].rearrange("p (g t) -> p g t", t=T), ACT.Ln, bias=zero[:]))
                    nc.scalar.activation(rinv[:], rinv[:], ACT.Exp, bias=zero[:], scale=-1.0).then_inc(S["rinv"], 1)
                    norm("mo", acen[:], asq[:], ab[:, T:2 * T], alnv[:], eps_ln[:], ars[:])
                    close()

            @block.vector
            def _(dve):
                with dve.Fori(0, B) as i:
                    wait = waits(dve, i)
                    link, close = chained(dve, wait, "chv")
                    tt, ts, stt = nc.vector.tensor_tensor, nc.vector.tensor_scalar, nc.vector.scalar_tensor_tensor

                    def center(tag, source, mean, centered):
                        wait(f"{tag}_mean")
                        tt(centered, source, mean, ALU.subtract).then_inc(S[f"{tag}_cen"], 1)

                    def normed(tag, centered, scale):
                        wait(f"{tag}_cen")
                        wait(f"{tag}_rs")
                        link(tt(centered, centered, scale, ALU.mult))

                    wait("cur")
                    center("ln1", x_cur[:], mixb[:, 0:T], cen[:])
                    normed("ln1", cen[:], rs[:])
                    ts(h1[:], cen[:], mod[:, 1:2], mod[:, 0:1], ALU.mult, ALU.add).then_inc(S["h1"], 1)
                    wait("xp")
                    for tap in range(TAPS):
                        for j in range(NH):
                            src = xp[:, j, tap:tap + T]
                            if tap == 0:
                                ins = ts(pz[:, j], src, w_conv[:, j, 0:1], b_conv[:, j:j + 1], ALU.mult, ALU.add)
                            else:
                                ins = stt(pz[:, j], src, w_conv[:, j, tap:tap + 1], pz[:, j], ALU.mult, ALU.add)
                        link(ins)
                    wait("z")
                    ts(pm[:], pz[:], LEAST, None, ALU.max).then_inc(S["cut"], 1)
                    wait("sig")
                    tt(sil[:], pz[:], pm[:], ALU.mult).then_inc(S["silu"], 1)
                    wait("dbl")
                    nc.vector.tensor_copy(rank_s[:], mixb[0:R, T:2 * T]).then_inc(S["rank"], 1)
                    link(nc.vector.tensor_copy(bc_v[:], mixb[0:96, 0:T]))
                    link(nc.vector.tensor_copy(bc[:], bc_v[:]))
                    link(tt(bc_r[0:64], bc_v[0:64], bc[0:64], ALU.subtract))
                    link(nc.vector.tensor_copy(bc[0:64], bc_r[0:64]))
                    link(tt(bc_r[0:32], bc_r[0:32], bc[0:32], ALU.subtract))
                    nc.vector.tensor_copy(bc[0:32], bc_r[0:32]).then_inc(S["bc"], 1)
                    wait("softp")
                    for j in range(NH):
                        last = ts(sp_r[:, j], mixb[:, j * T:(j + 1) * T], b_dt[:, j:j + 1], 0.0, ALU.add, ALU.max)
                    link(last)
                    stt(dt_s[:], sp_a[:], 1e-4, sp_r[:], ALU.add, ALU.add).then_inc(S["dt"], 1)
                    wait("dt")
                    link(tt(u_s[:], dt_s[:], sil[:, 0:NH], ALU.mult))
                    Hv = [t[:].rearrange("p (j n) t -> p j n t", j=NH) for t in H]
                    for g in range(NU):
                        b = g % 2
                        if g >= 2:
                            wait("ysum", g - 1)
                        else:
                            wait("ysum", 0)
                        for q in range(2):
                            wait("Bb", 2 * g + q + 1)
                            r = ring[q][:].rearrange("p (n t) -> p n t", t=T)
                            for j in range(NH):
                                last = tt(Hv[b][:, j, 2 * q:2 * q + 2], u_s[:, j:j + 1].to_broadcast([P, 2, T]), r, ALU.mult)
                            last.then_inc(S["Bused"], 1)
                        wait("Bused", 2 * g + 2)
                        wait("dA", g + 1)
                        flat = H[b][:].rearrange("p z t -> p (z t)")
                        nc.vector.tensor_tensor_scan(flat, dA[b][:].rearrange("p z t -> p (z t)"), flat, 0.0,
                                                     ALU.mult, ALU.add).then_inc(S["scan"], 1)
                        wait("scan", g + 1)
                        for q in range(2):
                            wait("Cb", 2 * g + q + 1)
                            r = ring[q][:].rearrange("p (n t) -> p n t", t=T)
                            for j in range(NH):
                                h = Hv[b][:, j, 2 * q:2 * q + 2]
                                last = tt(h, h, r, ALU.mult)
                            last.then_inc(S["hc"], 1)
                    wait("ysum", NU)
                    for j in range(NH):
                        last = stt(y_s[:, j], sil[:, j], skip[:, j:j + 1], ybank[:, j * T:(j + 1) * T], ALU.mult, ALU.add)
                    last.then_inc(S["yraw"], 1)
                    wait("yraw")
                    tt(y_s[:], y_s[:], sil[:, NH:], ALU.mult).then_inc(S["rms_cen"], 1)
                    wait("rms_cen")
                    wait("rms_rs")
                    for j in range(NH):
                        last = stt(y_s[:, j], y_s[:, j], rms_w[:, j:j + 1], rs[:], ALU.mult, ALU.mult)
                    last.then_inc(S["yout"], 1)
                    wait("mix")
                    stt(x1[:], mixb[:, 0:T], mod[:, 2:3], x_cur[:], ALU.mult, ALU.add).then_inc(S["x1"], 1)
                    wait("x1")
                    center("ln2", x1[:], mixb[:, 0:T], cen[:])
                    normed("ln2", cen[:], rs[:])
                    ts(h2[:], cen[:], mod[:, 4:5], mod[:, 3:4], ALU.mult, ALU.add).then_inc(S["h2"], 1)
                    wait("h2")
                    center("at", h2[:], ab[:, 0:T], acen[:])
                    normed("at", acen[:], ars[:])
                    ts(hn[:], acen[:], ln[:, 0:1], ln[:, 1:2], ALU.mult, ALU.add).then_inc(S["hn"], 1)
                    wait("v")
                    nc.vector.tensor_copy(vA[:, :, :, 0:DK], ab[:, 0:NC * D].rearrange("p (c h k) -> p c h k", c=NC, k=DK)).then_inc(S["vc"], 1)
                    for f in range(FILLS):
                        c, gp, j = f // 8, f // 4 % 2, f % 4
                        wait("smax", f + 1)
                        nc.vector.tensor_reduce(mxp[:, c, 2 * gp:2 * gp + 2, 32 * j + DK], sbank[f % 2][:].rearrange("p (g m) -> p g m", m=T),
                                                AX.X, ALU.max).then_inc(S["mx"], 1)
                    wait("mxT")
                    for half in range(2):
                        last = tt(qP[:, 2 * half:2 * half + 2], qP[:, 2 * half:2 * half + 2],
                                  av[half][:].rearrange("p (g t) -> p g t", t=T), ALU.add)
                    last.then_inc(S["qm"], 1)
                    wait("rinv")
                    tt(yh[:], yh[:], rinv[:], ALU.mult).then_inc(S["yn"], 1)
                    wait("proj")
                    tt(x2[:], h2[:], ab[:, 0:T], ALU.add).then_inc(S["x2"], 1)
                    wait("x2")
                    center("mo", x2[:], ab[:, 0:T], acen[:])
                    normed("mo", acen[:], ars[:])
                    ts(xf_all[:, bass.ds(i, 1), :].rearrange("p a t -> p (a t)"), acen[:], ln[:, 2:3], ln[:, 3:4], ALU.mult, ALU.add).then_inc(S["xf"], 1)
                    stt(x_all[:, bass.ds(i, 1), :].rearrange("p a t -> p (a t)"), x2[:], mod[:, 5:6], x1[:], ALU.mult, ALU.add).then_inc(S["fin"], 1)
                    close()

            @block.tensor
            def _(pe):
                with pe.Fori(0, B) as i:
                    wait = waits(pe, i)
                    mm = nc.tensor.matmul

                    def stats(tag, source, bank, parts=1, weights=mean_d):
                        wait(f"{tag}_sq")
                        for j in range(parts):
                            last = mm(bank[:, T:2 * T], weights[:], source[j], start=j == 0, stop=j == parts - 1)
                        last.then_inc(S[f"{tag}_var"], 1)

                    wait("cur")
                    wait("ln2_rs", 0)
                    wait("ln2_cen", 0)
                    mm(mixb[:, 0:T], mean_d[:], x_cur[:], start=True, stop=True).then_inc(S["ln1_mean"], 1)
                    stats("ln1", [sq[:, 0]], mixb)
                    wait("h1")
                    for j in range(NH):
                        last = mm(mixb[:, j * T:(j + 1) * T], w_inT[:, j * P:(j + 1) * P], h1[:], start=True, stop=True)
                    last.then_inc(S["xz_x"], 1)
                    wait("xp")
                    for j in range(NH):
                        last = mm(mixb[:, j * T:(j + 1) * T], w_inT[:, (NH + j) * P:(NH + j + 1) * P], h1[:], start=True, stop=True)
                    last.then_inc(S["xz_z"], 1)
                    wait("silu")
                    for j in range(NH):
                        mm(mixb[0:96, 0:T], w_dbl[:, j], sil[:, j], start=j == 0, stop=j == NH - 1)
                    for j in range(NH):
                        last = mm(mixb[0:R, T:2 * T], w_rank[:, j], sil[:, j], start=j == 0, stop=j == NH - 1)
                    last.then_inc(S["dbl"], 1)
                    wait("bc")
                    for j in range(NH):
                        last = mm(mixb[:, j * T:(j + 1) * T], w_dtT[:, j * P:(j + 1) * P], rank_s[:], start=True, stop=True)
                    last.then_inc(S["dtp"], 1)

                    def broadcast(name, g, q, first):
                        for n in range(2):
                            last = mm(ring[q][:, n * T:(n + 1) * T], pick[:, first + g * U + 2 * q + n], bc[:], start=True, stop=True)
                        last.then_inc(S[name], 1)

                    def sum_states(g):
                        hv = H[g % 2][:].rearrange("p (j n) t -> p n j t", j=NH)
                        wait("hc", 2 * g + 2)
                        for n in range(U):
                            last = mm(ybank[:], ident[:], hv[:, n], start=g == 0 and n == 0, stop=g == NU - 1 and n == U - 1)
                        last.then_inc(S["ysum"], 1)

                    for g in range(NU):
                        for q in range(2):
                            wait("hc", 2 * g - 2 + q + 1 if g else 0)
                            broadcast("Bb", g, q, 0)
                        for q in range(2):
                            wait("Bused", 2 * g + q + 1)
                            broadcast("Cb", g, q, NS)
                        if g:
                            sum_states(g - 1)
                    sum_states(NU - 1)
                    stats("rms", [sq[:, j] for j in range(NH)], mixb, NH, mean_i)
                    wait("yout")
                    for j in range(NH):
                        last = mm(mixb[:, 0:T], w_outT[:, j], y_s[:, j], start=j == 0, stop=j == NH - 1)
                    last.then_inc(S["mix"], 1)
                    wait("x1")
                    mm(mixb[:, 0:T], mean_d[:], x1[:], start=True, stop=True).then_inc(S["ln2_mean"], 1)
                    stats("ln2", [sq[:, 0]], mixb)
                    wait("h2")
                    wait("mo_rs", 0)
                    mm(ab[:, 0:T], mean_d[:], h2[:], start=True, stop=True).then_inc(S["at_mean"], 1)
                    stats("at", [asq[:]], ab)
                    wait("hn")
                    for name, w, done in (("q", w_q, None), ("k", w_k, "qc")):
                        for half in range(2):
                            if done:
                                wait(done, half + 1)
                            for g in range(2):
                                last = mm(av[half][:, g * T:(g + 1) * T], w[:, 2 * half + g], hn[:], start=True, stop=True)
                            last.then_inc(S[name], 1)
                    wait("kc", 2)
                    for c in range(NC):
                        last = mm(ab[:, c * D:(c + 1) * D], hn[:, c * P:(c + 1) * P], w_v[:], start=True, stop=True)
                    last.then_inc(S["v"], 1)
                    for f in range(FILLS):
                        c, gp, j = f // 8, f // 4 % 2, f % 4
                        if f >= 2:
                            wait("mx", f - 1)
                        else:
                            wait("pt", 0)
                        rows = slice(32 * j, 32 * j + DK)
                        for g in range(2):
                            last = mm(sbank[f % 2][:, g * T:(g + 1) * T], qP[rows, 2 * gp + g, c * P:(c + 1) * P],
                                      kP[rows, 2 * gp + g, :], start=True, stop=True)
                        last.then_inc(S["smax"], 1)
                    wait("mx", FILLS)
                    wait("vc")
                    for g in range(NG):
                        for c in range(NC):
                            last = nc.tensor.transpose(av[g // 2][:, (g % 2) * T + c * P:(g % 2) * T + (c + 1) * P], mxp[:, c, g], ident[:])
                    last.then_inc(S["mxT"], 1)
                    wait("qm")

                    def weigh(f):
                        g, j = f // 4, f % 4
                        wait("pt", f + 1)
                        for c in range(NC):
                            last = mm(av[g // 2][32 * j:32 * j + 32, (g % 2) * T:(g % 2 + 1) * T], vA[:, c, f], PT[:, f % RD, c],
                                      start=c == 0, stop=c == NC - 1, tile_position=(0, 32 * j))
                        if f % 8 == 7:
                            last.then_inc(S["pv"], 1)

                    for f in range(FILLS):
                        g, j = f // 4, f % 4
                        rows = slice(32 * j, 32 * j + DK + 1)
                        if f >= 2:
                            wait("pt", f - 1)
                        for c in range(NC):
                            last = mm(sbank[f % 2][:, c * T:(c + 1) * T], kP[rows, g, c * P:(c + 1) * P], qP[rows, g, :], start=True, stop=True)
                        last.then_inc(S["st"], 1)
                        if f >= 1:
                            weigh(f - 1)
                    weigh(FILLS - 1)
                    for half in range(2):
                        wait("pvc", half + 1)
                        for g in range(2):
                            last = mm(av[half][:, g * T:(g + 1) * T], spread[:], yh[:, 2 * half + g], start=True, stop=True)
                        last.then_inc(S["den"], 1)
                    wait("yn")
                    for g in range(NG):
                        last = mm(ab[:, 0:T], w_proj[:, g], yh[:, g], start=g == 0, stop=g == NG - 1)
                    last.then_inc(S["proj"], 1)
                    wait("x2")
                    mm(ab[:, 0:T], mean_d[:], x2[:], start=True, stop=True).then_inc(S["mo_mean"], 1)
                    stats("mo", [asq[:]], ab)

        with nc.Block() as block:
            @block.sync
            def _(sp):
                with sp.Fori(0, B) as i:
                    wait = waits(sp, i)
                    wait("m_out")
                    sp.dma_start(out[bass.ds(i, 1)].rearrange("a d t -> (a d) t"), ot[0]).then_inc(s_store, 16)
                sp.wait_ge(s_store, 16 * B + 16)

            @block.gpsimd
            def _(pool):
                with pool.Fori(0, B) as i:
                    wait = waits(pool, i)
                    wait("m_xm", 0)
                    nc.gpsimd.tensor_copy(xfc, xf_all[:, bass.ds(i, 1), :].rearrange("p a t -> p (a t)")).then_inc(S["m_x"], 1)

            @block.scalar
            def _(act):
                with act.Fori(0, B) as i:
                    wait = waits(act, i)
                    for f in range(NP_):
                        wait("m_up", f + 1)
                        nc.scalar.activation(gel[f % 4], banks[f % 4][:].rearrange("p (c t) -> p c t", t=T),
                                             ACT.Gelu_apprx_tanh, bias=zero[:]).then_inc(S["m_gel"], 1)

            @block.vector
            def _(dve):
                with dve.Fori(0, B) as i:
                    wait = waits(dve, i)
                    link, close = chained(dve, wait, "m_chv")
                    wait("m_lg")
                    link(nc.vector.tensor_copy(lg[:], ab[:, 0:NC * E].rearrange("p (c e) -> p c e", e=E)))
                    link(nc.vector.tensor_reduce(top[:, 0], lg[:], AX.X, ALU.max))
                    for c in range(NC):
                        last = nc.vector.scalar_tensor_tensor(key[:, c], lg[:, c], top[:, 0, c:c + 1], rank_e[:], ALU.is_equal, ALU.mult)
                    link(last)
                    link(nc.vector.tensor_reduce(top[:, 1], key[:], AX.X, ALU.max))
                    for c in range(NC):
                        last = nc.vector.tensor_scalar(hot[:, c], key[:, c], top[:, 1, c:c + 1], None, ALU.is_equal)
                    last.then_inc(S["m_hot"], 1)
                    for k in range(E // 2):
                        wait("m_mask", k + 1)
                        nc.vector.tensor_tensor(xm[:, 2 * k:2 * k + 2], xfc.rearrange("p (a t) -> p a t", a=1).to_broadcast([P, 2, T]),
                                                sbank[k % 2][:].rearrange("p (e t) -> p e t", t=T), ALU.mult).then_inc(S["m_xm"], 1)
                    wait("m_y")
                    link(nc.vector.tensor_copy(mod[:], mods[:, :, bass.ds(i, 1)].rearrange("p m a -> p (m a)")))
                    dve.wait_ge(s_store, i * 16 + 16)
                    nc.vector.scalar_tensor_tensor(ot[0], ybank[:, 0:T], mod[:, 5:6], x_all[:, bass.ds(i, 1), :].rearrange("p a t -> p (a t)"), ALU.mult, ALU.add).then_inc(S["m_out"], 1)
                    close()

            @block.tensor
            def _(pe):
                with pe.Fori(0, B) as i:
                    wait = waits(pe, i)
                    mm = nc.tensor.matmul
                    wait("m_x")
                    for c in range(NC):
                        mm(ab[:, c * E:(c + 1) * E], xfc[:, c * P:(c + 1) * P], gate_w[:], start=True, stop=False)
                        last = mm(ab[:, c * E:(c + 1) * E], ones_row[:], gate_b[:], start=False, stop=True)
                    last.then_inc(S["m_lg"], 1)
                    wait("m_hot")
                    wait("m_gel", 0)
                    for k in range(E // 2):
                        if k >= 2:
                            wait("m_xm", k - 1)
                        for e in range(2):
                            for c in range(NC):
                                last = mm(sbank[k % 2][:, e * T + c * P:e * T + (c + 1) * P],
                                          hot[:, c, 2 * k + e:2 * k + e + 1].to_broadcast([P, P]), ident_b[:], start=True, stop=True)
                        last.then_inc(S["m_mask"], 1)
                    wait("m_out", 0)

                    def down(f):
                        wait("m_gel", f + 1)
                        for c in range(2):
                            h = 2 * f + c
                            last = mm(ybank[:, 0:T], w2[:, h // HC, h % HC], gel[f % 4][:, c], start=h == 0, stop=h == E * HC - 1)
                        if f == NP_ - 1:
                            last.then_inc(S["m_y"], 1)

                    wait("m_xm", E // 2)
                    for f in range(NP_):
                        if f >= 4:
                            wait("m_gel", f - 3)
                        for c in range(2):
                            h = 2 * f + c
                            last = mm(banks[f % 4][:, c * T:(c + 1) * T], w1[:, h // HC, (h % HC) * P:(h % HC + 1) * P], xm[:, h // HC], start=True, stop=True)
                        last.then_inc(S["m_up"], 1)
                        if f >= 2:
                            down(f - 2)
                    down(NP_ - 2)
                    down(NP_ - 1)


def kernel(**inputs):
    import numpy as np
    import concourse.bacc as bacc
    from concourse import mybir as mb
    from concourse.bass_utils import run_bass_kernel_spmd as run

    a = {k: np.asarray(v) for k, v in inputs.items()}
    f32 = a["L0_attn_x"].dtype
    P, DK, GH, ROWS = 128, 8, 4, 32

    def halves(v):
        return v.reshape((2, P) + v.shape[1:]).swapaxes(0, 1)

    w_xT = a["L0_attn_W_x"].T
    rank = a["L0_attn_W_dt"].shape[1]
    bc_cols = w_xT[:, rank:]

    def spread_heads(w):
        o = np.zeros((w.shape[0], w.shape[1] // DK // GH, GH, ROWS), f32)
        o[..., :DK] = w.reshape(w.shape[0], -1, GH, DK)
        return o.reshape(w.shape[0], -1, GH * ROWS)

    qkv = a["L0_ffn_w_qkv"]
    D = qkv.shape[0]
    data = {
        "x": a["L0_attn_x"].transpose(0, 2, 1),
        "w_inT": a["L0_attn_W_in"].T,
        "w_conv": halves(a["L0_attn_W_conv"]),
        "b_conv": halves(a["L0_attn_b_conv"]),
        "w_dbl": halves(np.concatenate([bc_cols, bc_cols, bc_cols], axis=1)),
        "w_rank": halves(w_xT[:, :rank]),
        "w_dtT": a["L0_attn_W_dt"].T,
        "b_dt": halves(a["L0_attn_b_dt"]),
        "a_log": halves(a["L0_attn_A_log"]),
        "skip": halves(a["L0_attn_D"]),
        "rms_w": halves(a["L0_attn_rms_w"]),
        "w_outT": halves(a["L0_attn_W_out"].T),
        "ln": np.stack([a["L0_ffn_ln1_w"], a["L0_ffn_ln1_b"], a["L0_ffn_ln2_w"], a["L0_ffn_ln2_b"]], axis=1),
        "w_q": spread_heads(qkv[:, :D]),
        "w_k": spread_heads(qkv[:, D:2 * D]),
        "w_v": qkv[:, 2 * D:],
        "w_proj": spread_heads(a["L0_ffn_w_proj"].T).transpose(2, 1, 0),
        "gate_w": a["L0_ffn_gate_w"],
        "gate_b": a["L0_ffn_gate_b"][None],
        "w1": a["L0_ffn_w1"],
        "w2": a["L0_ffn_w2"],
        "cT": a["L0_c"].T,
        "w_mod": a["L0_wmod"].reshape(D, 6, D),
    }
    nc = bacc.Bacc("TRN2", target_bir_lowering=False, num_devices=1)
    arrays, io = {}, {}
    for name, v in data.items():
        v = np.ascontiguousarray(v)
        arrays[f"in_{name}"] = v
        io[name] = nc.dram_tensor(f"in_{name}", v.shape, mb.dt.from_np(v.dtype), kind="ExternalInput").ap()
    out = nc.dram_tensor("out_0", data["x"].shape, mb.dt.float32, kind="ExternalOutput").ap()
    adaln_block(nc, io, out)
    r = run(nc, [arrays], core_ids=[0])
    return np.ascontiguousarray(r.results[0]["out_0"].transpose(0, 2, 1))
```

```python
import concourse.bass as bass
from concourse import mybir
from contextlib import ExitStack


def adaln_block(nc, io, out):
    fp32 = mybir.dt.float32
    bf16 = mybir.dt.bfloat16
    ALU = mybir.AluOpType
    ACT = mybir.ActivationFunctionType
    AX = mybir.AxisListType

    B, D, T = io["x"].shape
    P = 128
    NH = io["w_inT"].shape[1] // P // 2
    NS = io["a_log"].shape[2]
    TAPS = io["w_conv"].shape[2]
    R = io["w_dtT"].shape[0]
    DK = 8
    NHD = D // DK
    HS = NHD // 2
    E = io["gate_w"].shape[1]
    HC = io["w1"].shape[2] // P
    NC = T // P
    U = 4
    NU = NS // U
    ZU = NH * U
    FILLS = NHD
    SLOTS = [(0, 0), (0, 1), (0, 2), (1, 0), (1, 1), (2, 0)]
    KR = len(SLOTS) * DK
    V1 = DK + 1
    LEAST = -43.0
    RD = 4
    assert D == P and NC * P == T and NC == 2 and NS % U == 0 and U == 4

    ctx = ExitStack()
    with ctx:
        def sb(name, shape, dt=fp32):
            return ctx.enter_context(nc.sbuf_tensor(name, shape, dt))

        per = {}
        S = {}

        def event(name, times=1):
            S[name] = ctx.enter_context(nc.semaphore(name))
            per[name] = times

        w_inT = sb("w_inT", [P, 2 * NH * P])
        w_conv = sb("w_conv", [P, NH, TAPS])
        b_conv = sb("b_conv", [P, NH])
        w_dbl = sb("w_dbl", [P, NH, 3 * 2 * NS])
        w_rank = sb("w_rank", [P, NH, R])
        w_dtT = sb("w_dtT", [R, NH * P])
        b_dt = sb("b_dt", [P, NH])
        a_neg = sb("a_neg", [P, NH, NS])
        a_log = sb("a_log", [P, NH, NS])
        skip = sb("skip", [P, NH])
        rms_w = sb("rms_w", [P, NH])
        w_outT = sb("w_outT", [P, NH, D])
        ln = sb("ln", [P, 4])
        w_q = sb("w_q", [P, D])
        w_k = sb("w_k", [P, D])
        w_v = sb("w_v", [P, D])
        w_proj = sb("w_proj", [P, D])
        gate_w = sb("gate_w", [P, E])
        gate_b = sb("gate_b", [1, E])
        w1 = sb("w1", [P, E, HC * P])
        w2 = sb("w2", [P, E, HC, D])
        cT = sb("cT", [P, B])
        w_mod = sb("w_mod", [P, 6, P])
        c_tmp = sb("c_tmp", [P, 3, B])
        mods = sb("mods", [P, 6, B])
        mods_abs = sb("mods_abs", [P, 2, B])
        ident = sb("ident", [P, P])
        ident_b = sb("ident_b", [P, P], bf16)
        mean_d = sb("mean_d", [P, P])
        mean_i = sb("mean_i", [P, P])
        pick = sb("pick", [96, 2 * NS, P], bf16)
        ones_row = sb("ones_row", [1, P])
        eps_ln = sb("eps_ln", [P, 1])
        eps_rms = sb("eps_rms", [P, 1])
        one = sb("one", [P, 1])
        zero = sb("zero", [P, 1])
        zeros = sb("zeros", [P, ZU, 1])
        rank_e = sb("rank_e", [P, E])

        x_all = sb("x_all", [P, B, T])
        xf_all = sb("xf_all", [P, B, T])

        mod_p = sb("mod_p", [P, 2])
        pcen = sb("pcen", [P, T])
        psq = sb("psq", [P, T])
        prs = sb("prs", [P, T])
        h1 = sb("h1", [P, T])
        xp = sb("xp", [P, NH, TAPS - 1 + T])
        pz = sb("pz", [P, 2 * NH, T])
        pm = sb("pm", [P, 2 * NH, T])
        sil = sb("sil", [P, 2 * NH, T])
        rank_s = sb("rank_s", [R, T])
        bc_v = sb("bc_v", [96, T])
        bc = sb("bc", [96, T], bf16)
        sp_a = sb("sp_a", [P, NH, T])
        sp_r = sb("sp_r", [P, NH, T])
        dt_s = sb("dt_s", [P, NH, T])
        u_s = sb("u_s", [P, NH, T])
        dA = [sb(f"dA{k}", [P, ZU, T]) for k in range(2)]
        H = [sb(f"H{k}", [P, ZU, T]) for k in range(2)]
        mod_q = sb("mod_q", [P, 3])
        y_s = sb("y_s", [P, NH, T])
        qsq = sb("qsq", [P, NH, T])
        qrs = sb("qrs", [P, T])
        qcen = sb("qcen", [P, T])
        x1 = sb("x1", [P, T])
        h2 = sb("h2", [P, T])
        hn = sb("hn", [P, T])
        qk_r = sb("qk_r", [P, 2, T])
        qk_p = [sb(f"qk_p{k}", [P, 2, T], bf16) for k in range(3)]
        stack = sb("stack", [P, 2, HS, T], bf16)
        vA = sb("vA", [P, NC, NHD, V1])
        mx = sb("mx", [P, NC, NHD])
        mx_r = sb("mx_r", [NHD, T])
        mx_p = sb("mx_p", [NHD, 3, T], bf16)
        PT = sb("PT", [P, RD, NC, T])
        gb_f = sb("gb_f", [P, 1])
        rden = sb("rden", [P, NC, NHD])
        yn = sb("yn", [P, NC, D])
        ynT = sb("ynT", [P, T])
        x2 = sb("x2", [P, T])
        fcen = sb("fcen", [P, T])
        fsq = sb("fsq", [P, T])
        frs = sb("frs", [P, T])

        def bank(k):
            return ctx.enter_context(nc.psum_tensor(f"bank{k}", [P, 512], fp32))

        pb, ring0, ring1, yb, qb, fb, s0, s1 = [bank(k) for k in range(8)]
        ring = [ring0, ring1]
        sbank = [s0, s1]

        CONSTS = 5
        s_load = ctx.enter_context(nc.semaphore("s_load"))
        s_const = ctx.enter_context(nc.semaphore("s_const"))
        s_mod = ctx.enter_context(nc.semaphore("s_mod"))
        s_silc = ctx.enter_context(nc.semaphore("s_silc"))
        s_setup = ctx.enter_context(nc.semaphore("s_setup"))
        s_chain = ctx.enter_context(nc.semaphore("s_chain"))

        loads = [(x_all, io["x"].rearrange("b d t -> d b t")), (w_inT, io["w_inT"]), (w_conv, io["w_conv"]),
                 (b_conv, io["b_conv"]), (w_dbl, io["w_dbl"]), (w_rank, io["w_rank"]), (w_dtT, io["w_dtT"]),
                 (b_dt, io["b_dt"]), (a_log, io["a_log"]), (skip, io["skip"]), (rms_w, io["rms_w"]),
                 (w_outT, io["w_outT"]), (ln, io["ln"]), (w_q, io["w_q"]), (w_k, io["w_k"]), (w_v, io["w_v"]),
                 (w_proj, io["w_proj"]), (gate_w, io["gate_w"]), (gate_b, io["gate_b"]), (cT, io["cT"]),
                 (w_mod, io["w_mod"]), (w1, io["w1"].rearrange("e d h -> d e h")),
                 (w2, io["w2"].rearrange("e (c p) d -> p e c d", p=P))]

        with nc.Block() as block:
            @block.sync
            def _(sp):
                for tile, src in loads:
                    sp.dma_start(tile[:], src).then_inc(s_load, 16)
                sp.wait_ge(s_load, 16 * len(loads))

            @block.gpsimd
            def _(pool):
                nc.gpsimd.memset(ident[:], 0.0)
                nc.gpsimd.memset(mean_d[:], 1.0 / D)
                nc.gpsimd.memset(mean_i[:], 1.0 / (NH * P))
                nc.gpsimd.memset(pick[:], 0.0)
                nc.gpsimd.memset(ones_row[:], 1.0)
                nc.gpsimd.memset(eps_ln[:], 1e-5)
                nc.gpsimd.memset(eps_rms[:], 1e-6)
                nc.gpsimd.memset(one[:], 1.0)
                nc.gpsimd.memset(zero[:], 0.0)
                nc.gpsimd.memset(stack[:, 1], -1.0).then_inc(s_const, 1)
                pool.wait_ge(s_const, 1)
                nc.gpsimd.affine_select(out=ident[:], in_=ident[:], compare_op=ALU.not_equal, fill=1.0, base=0,
                                        pattern=[[-1, P]], channel_multiplier=1)
                count = 1
                for part in range(3):
                    nc.gpsimd.affine_select(out=pick[:], in_=pick[:], compare_op=ALU.not_equal, fill=1.0,
                                            base=-2 * NS * part, pattern=[[-1, 2 * NS], [0, P]],
                                            channel_multiplier=1).then_inc(s_const, 1)
                    count += 1
                    pool.wait_ge(s_const, count)
                nc.gpsimd.iota(rank_e[:], pattern=[[-1, E]], base=E, channel_multiplier=0,
                               allow_small_or_imprecise_dtypes=True)
                nc.gpsimd.tensor_copy(ident_b[:], ident[:]).then_inc(s_const, 1)
                assert count + 1 == CONSTS

            @block.scalar
            def _(act):
                nc.scalar.preload_act_table_set("natural_log_exp_and_others")
                act.wait_ge(s_load, 16 * len(loads))
                act.wait_ge(s_const, CONSTS)
                nc.scalar.activation(a_neg[:], a_log[:], ACT.Exp, bias=zero[:]).then_inc(s_silc, 1)
                act.wait_ge(s_mod, 1)
                nc.scalar.activation(c_tmp[:, 1], c_tmp[:, 0], ACT.Exp, bias=zero[:], scale=-1.0).then_inc(s_silc, 1)
                act.wait_ge(s_silc, 2)
                nc.scalar.activation(c_tmp[:, 2], c_tmp[:, 1], ACT.Ln, bias=one[:]).then_inc(s_silc, 1)
                act.wait_ge(s_silc, 3)
                nc.scalar.activation(c_tmp[:, 1], c_tmp[:, 2], ACT.Exp, bias=zero[:], scale=-1.0).then_inc(s_silc, 1)

            @block.vector
            def _(dve):
                count = 0

                def link(ins):
                    nonlocal count
                    count += 1
                    ins.then_inc(s_mod, 1)
                    dve.wait_ge(s_mod, count)

                dve.wait_ge(s_load, 16 * len(loads))
                link(nc.vector.tensor_scalar(c_tmp[:, 0], cT[:], LEAST, None, ALU.max))
                nc.vector.memset(xp[:, :, 0:TAPS - 1], 0.0)
                nc.vector.memset(vA[:, :, :, DK:V1], 1.0)
                nc.vector.memset(zeros[:], 0.0)
                dve.wait_ge(s_silc, 1)
                nc.vector.tensor_scalar(a_neg[:], a_neg[:], -1.0, None, ALU.mult)
                dve.wait_ge(s_silc, 4)
                link(nc.vector.tensor_tensor(c_tmp[:, 0], cT[:], c_tmp[:, 1], ALU.mult))
                dve.wait_ge(s_setup, 1)
                link(nc.vector.tensor_copy(mods[:], yb[:, 0:6 * B].rearrange("p (m b) -> p m b", b=B)))
                for m in (1, 4):
                    nc.vector.tensor_scalar(mods[:, m], mods[:, m], 1.0, None, ALU.add)
                for k, m in enumerate((2, 5)):
                    link(nc.vector.tensor_scalar(c_tmp[:, 1], mods[:, m], -1.0, None, ALU.mult))
                    link(nc.vector.tensor_tensor(mods_abs[:, k], mods[:, m], c_tmp[:, 1], ALU.max))
                    link(nc.vector.tensor_scalar(mods_abs[:, k], mods_abs[:, k], 0.25, None, ALU.max))
                    link(nc.vector.tensor_scalar(c_tmp[:, 2], mods[:, m], 0.0, 2.0, ALU.is_ge, ALU.mult))
                    link(nc.vector.tensor_scalar(c_tmp[:, 2], c_tmp[:, 2], -1.0, None, ALU.add))
                    link(nc.vector.tensor_tensor(mods[:, m], c_tmp[:, 2], mods_abs[:, k], ALU.mult))

            @block.tensor
            def _(pe):
                pe.wait_ge(s_mod, 2)
                for m in range(6):
                    last = nc.tensor.matmul(yb[:, m * B:(m + 1) * B], w_mod[:, m], c_tmp[:, 0],
                                            start=True, stop=True)
                last.then_inc(s_setup, 1)

        for tag in ("ln1", "rms", "ln2", "at", "mo"):
            for step in ("mean", "cen", "sq", "var", "rs"):
                event(f"{tag}_{step}")
        for name, times in (
                ("h1", 1), ("xz_x", 1), ("xp", 1), ("xz_z", 1), ("z", 1), ("cut", 1), ("sig", 1), ("silu", 1),
                ("dbl", 1), ("bc", 1), ("dtp", 1), ("softp", 1), ("dt", 1), ("u", 1),
                ("zp", NU), ("zv", NU), ("dA", NU), ("Bb", 2 * NU), ("Bused", 2 * NU), ("Cb", 2 * NU),
                ("hc", 2 * NU), ("scan", NU), ("ysum", NU),
                ("yraw", 1), ("yout", 1), ("mix", 1), ("x1", 1), ("h2", 1), ("hn", 1), ("qk", 1), ("hi", 1),
                ("r1", 1), ("mid", 1), ("lo", 1), ("v", 1), ("vc", 1),
                ("smax", FILLS), ("mx", FILLS), ("mxT", 1), ("mxp", 1),
                ("st", FILLS), ("pt", FILLS), ("pv", 1),
                ("yn", 1), ("ynT", 1), ("ynTc", 1), ("proj", 1), ("x2", 1), ("fin", 1),
                ("act_p", 5), ("act_q", 3), ("act_f", 1), ("dve_p", 11), ("dve_q", 3), ("dve_m", 3), ("dve_f", 3)):
            event(name, times)
        s_stack = ctx.enter_context(nc.semaphore("s_stack"))
        s_mrow = ctx.enter_context(nc.semaphore("s_mrow"))
        lg = sb("lg", [P, NC, E])
        key = sb("key", [P, NC, E])
        top = sb("top", [P, 2, NC])
        hot = sb("hot", [P, NC, E], bf16)
        xfc = H[0][:, 0]
        xm = dA[0]
        gel = [H[1][:, 2 * k:2 * k + 2] for k in range(4)]
        ot = [y_s[:, k] for k in range(2)]
        banks = [ring0, ring1, s0, s1]
        NP_ = E * HC // 2
        for name, times in (("m_x", 1), ("m_lg", 1), ("m_hot", 1), ("m_mask", E // 2), ("m_xm", E // 2),
                            ("m_up", NP_), ("m_gel", NP_), ("m_y", 1), ("m_out", 1), ("m_chv", 5)):
            event(name, times)
        s_store = ctx.enter_context(nc.semaphore("s_store"))

        def start_counts(sp):
            for name in per:
                sp.sem_inc(S[name], 1)
            sp.sem_inc(s_store, 16)

        def counts(eng, turn, shift=0):
            kept = {}

            def count(name, k=1):
                n = per[name]
                if isinstance(turn, int):
                    return (turn + shift) * n + k + 1
                if n not in kept:
                    kept[n] = turn if n == 1 else eng.snap(turn * n)
                return kept[n] + (shift * n + k + 1)
            return count

        def chained(eng, at, name):
            count = 0

            def link(ins):
                nonlocal count
                count += 1
                assert count <= per[name]
                ins.then_inc(S[name], 1)
                eng.wait_ge(S[name], at(name, count))

            def close():
                assert count == per[name], (name, count)
            link.close = close
            return link

        def pipeline(eng, turn):
            turn(-1, False, False, True)
            turn(0, True, False, True)
            with eng.Fori(1, B - 1) as k:
                turn(k, True, True, True)
            turn(B - 1, True, True, False)
            turn(B, False, True, False)

        def token_block(t, k, shift=0):
            return t[:, bass.ds(k + shift, 1), :].rearrange("p a t -> p (a t)")

        def column(t, m, n, k, shift=0):
            return t[:, m:m + n, bass.ds(k + shift, 1)].rearrange("p m a -> p (m a)")

        with nc.Block() as block:
            @block.sync
            def _(sp):
                start_counts(sp)

        ZP = U

        with nc.Block() as block:
            @block.sync
            def _(sp):
                def turn(k, scan, att, prep):
                    was = counts(sp, k, -1)
                    now = counts(sp, k)
                    if att:
                        sp.wait_ge(S["mxp"], was("mxp"))
                        for e in range(2):
                            for part in range(3):
                                row = 64 * e + KR + part
                                sp.dma_start(stack[row:row + 1, 0], mx_p[e * HS:(e + 1) * HS, part]).then_inc(s_mrow, 16)
                    if scan:
                        sp.wait_ge(S["lo"], now("lo"))
                        for qk in range(2):
                            for slot, parts in enumerate(SLOTS):
                                for e in range(2):
                                    row = 64 * e + slot * DK
                                    sp.dma_start(stack[row:row + DK, qk],
                                                 qk_p[parts[qk]][64 * e:64 * e + DK * HS, qk]).then_inc(s_stack, 16)
                pipeline(sp, turn)

            @block.gpsimd
            def _(pool):
                def turn(k, scan, att, prep):
                    now = counts(pool, k)
                    if scan:
                        pool.wait_ge(S["dt"], now("dt"))
                        for g in range(NU):
                            pool.wait_ge(S["scan"], now("scan", g - 1 if g >= 2 else 0))
                            nc.gpsimd.tensor_tensor(dA[g % 2][:, :, 0:1], zeros[:], zeros[:], ALU.add)
                            for z in range(ZP):
                                j, n = z // U, g * U + z % U
                                last = nc.gpsimd.tensor_scalar(dA[g % 2][:, z, 1:T], dt_s[:, j, 1:T],
                                                               a_neg[:, j, n:n + 1], -10.0, ALU.mult, ALU.max)
                            last.then_inc(S["zp"], 1)
                pipeline(pool, turn)

            @block.scalar
            def _(act):
                nc.scalar.preload_act_table_set("natural_log_exp_and_others")

                def turn(k, scan, att, prep):
                    now, was, then = counts(act, k), counts(act, k, -1), counts(act, k, 1)
                    two = "p (a t) -> p a t"

                    def square(at, tag, source, result):
                        act.wait_ge(S[f"{tag}_cen"], at(f"{tag}_cen"))
                        nc.scalar.activation(result, source, ACT.Square, bias=zero[:]).then_inc(S[f"{tag}_sq"], 1)

                    def inverse_root(at, link, tag, variance, eps, result):
                        act.wait_ge(S[f"{tag}_var"], at(f"{tag}_var"))
                        link(nc.scalar.activation(result, variance, ACT.Ln, bias=eps))
                        nc.scalar.activation(result, result, ACT.Exp, bias=zero[:], scale=-0.5).then_inc(S[f"{tag}_rs"], 1)

                    def weights(first, last):
                        for f in range(first, last):
                            act.wait_ge(S["st"], was("st", f + 1))
                            nc.scalar.activation(PT[:, f % RD], sbank[f % 2][:].rearrange(two, t=T), ACT.Exp,
                                                 bias=zero[:], scale=float(DK) ** -0.5).then_inc(S["pt"], 1)

                    link_p, link_q, link_f = chained(act, then, "act_p"), chained(act, now, "act_q"), chained(act, was, "act_f")
                    for g in range(NU):
                        if scan:
                            act.wait_ge(S["zp"], now("zp", g + 1))
                            act.wait_ge(S["zv"], now("zv", g + 1))
                            nc.scalar.activation(dA[g % 2][:, :, 1:T], dA[g % 2][:, :, 1:T], ACT.Exp,
                                                 bias=zero[:]).then_inc(S["dA"], 1)
                        if att and g >= 2:
                            weights((g - 2) * 8, (g - 1) * 8)
                    if prep:
                        square(then, "ln1", pcen[:], psq[:])
                    if scan:
                        square(now, "rms", y_s[:], qsq[:])
                    if att:
                        act.wait_ge(S["ynT"], was("ynT"))
                        nc.scalar.activation(ynT[:], fb[:, 0:T], ACT.Copy).then_inc(S["ynTc"], 1)
                    if prep:
                        inverse_root(then, link_p, "ln1", pb[:, T:2 * T], eps_ln[:], prs[:])
                    if scan:
                        inverse_root(now, link_q, "rms", yb[:, T:2 * T], eps_rms[:], qrs[:])
                    if prep:
                        act.wait_ge(S["xz_x"], then("xz_x"))
                        nc.scalar.activation(xp[:, :, TAPS - 1:], pb[:].rearrange(two, t=T), ACT.Copy).then_inc(S["xp"], 1)
                    if att:
                        square(was, "mo", fcen[:], fsq[:])
                    if prep:
                        act.wait_ge(S["xz_z"], then("xz_z"))
                        nc.scalar.activation(pz[:, NH:2 * NH], pb[:].rearrange(two, t=T), ACT.Copy).then_inc(S["z"], 1)
                    if scan:
                        square(now, "ln2", qcen[:], qsq[:, 0])
                    if att:
                        inverse_root(was, link_f, "mo", fb[:, T:2 * T], eps_ln[:], frs[:])
                        link_f.close()
                    if prep:
                        act.wait_ge(S["cut"], then("cut"))
                        link_p(nc.scalar.activation(pm[:], pm[:], ACT.Exp, bias=zero[:], scale=-1.0))
                        link_p(nc.scalar.activation(pm[:], pm[:], ACT.Ln, bias=one[:]))
                        nc.scalar.activation(pm[:], pm[:], ACT.Exp, bias=zero[:], scale=-1.0).then_inc(S["sig"], 1)
                    if scan:
                        inverse_root(now, link_q, "ln2", yb[:, T:2 * T], eps_ln[:], qrs[:])
                        square(now, "at", qcen[:], qsq[:, 1])
                        inverse_root(now, link_q, "at", yb[:, T:2 * T], eps_ln[:], qrs[:])
                    if prep:
                        act.wait_ge(S["dtp"], then("dtp"))
                        for j in range(NH):
                            last = nc.scalar.activation(sp_a[:, j], pb[:, j * T:(j + 1) * T], ACT.Abs, bias=b_dt[:, j:j + 1])
                        link_p(last)
                        link_p(nc.scalar.activation(sp_a[:], sp_a[:], ACT.Exp, bias=zero[:], scale=-1.0))
                        nc.scalar.activation(sp_a[:], sp_a[:], ACT.Ln, bias=one[:]).then_inc(S["softp"], 1)
                        link_p.close()
                    if scan:
                        act.wait_ge(S["qk"], now("qk"))
                        nc.scalar.activation(qk_p[0][:], qb[:].rearrange(two, t=T), ACT.Copy).then_inc(S["hi"], 1)
                        act.wait_ge(S["r1"], now("r1"))
                        nc.scalar.activation(qk_p[1][:], qk_r[:], ACT.Copy).then_inc(S["mid"], 1)
                        act.wait_ge(S["v"], now("v"))
                        nc.scalar.activation(vA[:, :, :, 0:DK], qb[:, 0:NC * D].rearrange("p (c h k) -> p c h k", c=NC, k=DK),
                                             ACT.Copy).then_inc(S["vc"], 1)
                        link_q.close()
                pipeline(act, turn)

            @block.vector
            def _(dve):
                tt, ts, stt = nc.vector.tensor_tensor, nc.vector.tensor_scalar, nc.vector.scalar_tensor_tensor
                Hv = [t[:].rearrange("p (j n) t -> p j n t", j=NH) for t in H]

                def turn(k, scan, att, prep):
                    now, was, then = counts(dve, k), counts(dve, k, -1), counts(dve, k, 1)
                    link_p, link_q = chained(dve, then, "dve_p"), chained(dve, now, "dve_q")
                    link_m, link_f = chained(dve, was, "dve_m"), chained(dve, was, "dve_f")

                    def center(at, tag, source, mean, centered):
                        dve.wait_ge(S[f"{tag}_mean"], at(f"{tag}_mean"))
                        tt(centered, source, mean, ALU.subtract).then_inc(S[f"{tag}_cen"], 1)

                    def normed(at, link, tag, centered, scale):
                        dve.wait_ge(S[f"{tag}_rs"], at(f"{tag}_rs"))
                        link(tt(centered, centered, scale, ALU.mult))

                    def exponents(g):
                        if g >= 2:
                            dve.wait_ge(S["scan"], now("scan", g - 1))
                        for z in range(ZP, ZU):
                            j, n = z // U, g * U + z % U
                            last = ts(dA[g % 2][:, z, 1:T], dt_s[:, j, 1:T], a_neg[:, j, n:n + 1], -10.0, ALU.mult, ALU.max)
                        last.then_inc(S["zv"], 1)

                    def inputs(g):
                        dve.wait_ge(S["ysum"], now("ysum", g - 1 if g >= 2 else 0))
                        for q in range(2):
                            dve.wait_ge(S["Bb"], now("Bb", 2 * g + q + 1))
                            r = ring[q][:].rearrange("p (n t) -> p n t", t=T)
                            for j in range(NH):
                                last = tt(Hv[g % 2][:, j, 2 * q:2 * q + 2], u_s[:, j:j + 1].to_broadcast([P, 2, T]), r, ALU.mult)
                            last.then_inc(S["Bused"], 1)

                    def states(g):
                        dve.wait_ge(S["Bused"], now("Bused", 2 * g + 2))
                        dve.wait_ge(S["dA"], now("dA", g + 1))
                        flat = H[g % 2][:].rearrange("p z t -> p (z t)")
                        nc.vector.tensor_tensor_scan(flat, dA[g % 2][:].rearrange("p z t -> p (z t)"), flat, 0.0,
                                                     ALU.mult, ALU.add).then_inc(S["scan"], 1)
                        dve.wait_ge(S["scan"], now("scan", g + 1))
                        for q in range(2):
                            dve.wait_ge(S["Cb"], now("Cb", 2 * g + q + 1))
                            r = ring[q][:].rearrange("p (n t) -> p n t", t=T)
                            for j in range(NH):
                                h = Hv[g % 2][:, j, 2 * q:2 * q + 2]
                                last = tt(h, h, r, ALU.mult)
                            last.then_inc(S["hc"], 1)

                    def maxima(first, last):
                        for f in range(first, last):
                            c, e, h = f // 8, f % 2, f // 2 % 4 * 2
                            dve.wait_ge(S["smax"], was("smax", f + 1))
                            nc.vector.tensor_reduce(mx[:, c, e * HS + h:e * HS + h + 2], sbank[f % 2][:].rearrange("p (g m) -> p g m", m=T),
                                                    AX.X, ALU.max).then_inc(S["mx"], 1)

                    def scaled_maxima():
                        dve.wait_ge(S["mxT"], was("mxT"))
                        link_m(nc.vector.tensor_copy(mx_p[:, 0], qb[0:NHD, 0:T]))
                        link_m(tt(mx_r[:], qb[0:NHD, 0:T], mx_p[:, 0], ALU.subtract))
                        link_m(nc.vector.tensor_copy(mx_p[:, 1], mx_r[:]))
                        tt(mx_p[:, 2], mx_r[:], mx_p[:, 1], ALU.subtract).then_inc(S["mxp"], 1)
                        link_m.close()

                    if scan:
                        exponents(0)
                        inputs(0)
                        exponents(1)
                    if att:
                        maxima(0, 4)
                    if scan:
                        states(0)
                    if att:
                        maxima(4, 10)
                    if scan:
                        inputs(1)
                        states(1)
                        exponents(2)
                    if att:
                        maxima(10, 16)
                        scaled_maxima()
                    if scan:
                        inputs(2)
                        states(2)
                        exponents(3)
                        inputs(3)
                        states(3)
                    if prep:
                        link_p(nc.vector.tensor_copy(mod_p[:], column(mods, 0, 2, k, 1)))
                        center(then, "ln1", token_block(x_all, k, 1), pb[:, 0:T], pcen[:])
                    if scan:
                        dve.wait_ge(S["ysum"], now("ysum", NU))
                        for j in range(NH):
                            last = stt(y_s[:, j], sil[:, j], skip[:, j:j + 1], yb[:, j * T:(j + 1) * T], ALU.mult, ALU.add)
                        last.then_inc(S["yraw"], 1)
                        link_q(nc.vector.tensor_copy(mod_q[:], column(mods, 2, 3, k)))
                        dve.wait_ge(S["yraw"], now("yraw"))
                        tt(y_s[:], y_s[:], sil[:, NH:], ALU.mult).then_inc(S["rms_cen"], 1)
                    if att:
                        dve.wait_ge(S["pv"], was("pv"))
                        sums = fb[:, 0:NC * NHD * V1].rearrange("p (c h v) -> p c h v", c=NC, v=V1)
                        link_f(nc.vector.reciprocal(rden[:], sums[:, :, :, DK]))
                        for c in range(NC):
                            last = tt(yn[:, c].rearrange("p (h v) -> p h v", v=DK), sums[:, c, :, 0:DK],
                                      rden[:, c].rearrange("p (h a) -> p h a", a=1).to_broadcast([P, NHD, DK]), ALU.mult)
                        last.then_inc(S["yn"], 1)
                    if prep:
                        normed(then, link_p, "ln1", pcen[:], prs[:])
                        ts(h1[:], pcen[:], mod_p[:, 1:2], mod_p[:, 0:1], ALU.mult, ALU.add).then_inc(S["h1"], 1)
                    if scan:
                        dve.wait_ge(S["rms_cen"], now("rms_cen"))
                        dve.wait_ge(S["rms_rs"], now("rms_rs"))
                        for j in range(NH):
                            last = stt(y_s[:, j], y_s[:, j], rms_w[:, j:j + 1], qrs[:], ALU.mult, ALU.mult)
                        last.then_inc(S["yout"], 1)
                    if att:
                        dve.wait_ge(S["proj"], was("proj"))
                        tt(x2[:], h2[:], fb[:, 0:T], ALU.add).then_inc(S["x2"], 1)
                        link_f(nc.vector.tensor_copy(gb_f[:], column(mods, 5, 1, k, -1)))
                    if scan:
                        dve.wait_ge(S["mix"], now("mix"))
                        stt(x1[:], yb[:, 0:T], mod_q[:, 0:1], token_block(x_all, k), ALU.mult, ALU.add).then_inc(S["x1"], 1)
                    if att:
                        dve.wait_ge(S["x2"], was("x2"))
                        center(was, "mo", x2[:], fb[:, 0:T], fcen[:])
                    if prep:
                        dve.wait_ge(S["xp"], then("xp"))
                        for tap in range(TAPS):
                            for j in range(NH):
                                src = xp[:, j, tap:tap + T]
                                if tap == 0:
                                    ins = ts(pz[:, j], src, w_conv[:, j, 0:1], b_conv[:, j:j + 1], ALU.mult, ALU.add)
                                else:
                                    ins = stt(pz[:, j], src, w_conv[:, j, tap:tap + 1], pz[:, j], ALU.mult, ALU.add)
                            link_p(ins)
                        dve.wait_ge(S["z"], then("z"))
                        ts(pm[:], pz[:], LEAST, None, ALU.max).then_inc(S["cut"], 1)
                    if scan:
                        dve.wait_ge(S["x1"], now("x1"))
                        center(now, "ln2", x1[:], yb[:, 0:T], qcen[:])
                        nc.vector.tensor_copy(token_block(x_all, k), x1[:])
                    if att:
                        normed(was, link_f, "mo", fcen[:], frs[:])
                        ts(token_block(xf_all, k, -1), fcen[:], ln[:, 2:3], ln[:, 3:4], ALU.mult, ALU.add)
                        stt(token_block(x_all, k, -1), x2[:], gb_f[:], token_block(x_all, k, -1), ALU.mult, ALU.add).then_inc(S["fin"], 1)
                        link_f.close()
                    if scan:
                        normed(now, link_q, "ln2", qcen[:], qrs[:])
                        ts(h2[:], qcen[:], mod_q[:, 2:3], mod_q[:, 1:2], ALU.mult, ALU.add).then_inc(S["h2"], 1)
                        dve.wait_ge(S["h2"], now("h2"))
                        center(now, "at", h2[:], yb[:, 0:T], qcen[:])
                    if prep:
                        dve.wait_ge(S["sig"], then("sig"))
                        tt(sil[:], pz[:], pm[:], ALU.mult).then_inc(S["silu"], 1)
                        dve.wait_ge(S["dbl"], then("dbl"))
                        nc.vector.tensor_copy(rank_s[:], pb[0:R, T:2 * T])
                        link_p(nc.vector.tensor_copy(bc[:], pb[0:96, 0:T]))
                        link_p(tt(bc_v[0:64], pb[0:64, 0:T], bc[0:64], ALU.subtract))
                        link_p(nc.vector.tensor_copy(bc[0:64], bc_v[0:64]))
                        link_p(tt(bc_v[0:32], bc_v[0:32], bc[0:32], ALU.subtract))
                        nc.vector.tensor_copy(bc[0:32], bc_v[0:32]).then_inc(S["bc"], 1)
                    if scan:
                        normed(now, link_q, "at", qcen[:], qrs[:])
                        ts(hn[:], qcen[:], ln[:, 0:1], ln[:, 1:2], ALU.mult, ALU.add).then_inc(S["hn"], 1)
                    if prep:
                        dve.wait_ge(S["softp"], then("softp"))
                        for j in range(NH):
                            last = ts(sp_r[:, j], pb[:, j * T:(j + 1) * T], b_dt[:, j:j + 1], 0.0, ALU.add, ALU.max)
                        link_p(last)
                        stt(dt_s[:], sp_a[:], 1e-4, sp_r[:], ALU.add, ALU.add).then_inc(S["dt"], 1)
                        dve.wait_ge(S["dt"], then("dt"))
                        tt(u_s[:], dt_s[:], sil[:, 0:NH], ALU.mult).then_inc(S["u"], 1)
                        dve.wait_ge(S["u"], then("u"))
                        link_p.close()
                    if scan:
                        dve.wait_ge(S["hi"], now("hi"))
                        tt(qk_r[:], qb[:].rearrange("p (a t) -> p a t", t=T), qk_p[0][:], ALU.subtract).then_inc(S["r1"], 1)
                        dve.wait_ge(S["mid"], now("mid"))
                        tt(qk_p[2][:], qk_r[:], qk_p[1][:], ALU.subtract).then_inc(S["lo"], 1)
                        link_q.close()
                pipeline(dve, turn)

            @block.tensor
            def _(pe):
                mm = nc.tensor.matmul

                def turn(k, scan, att, prep):
                    now, was, then = counts(pe, k), counts(pe, k, -1), counts(pe, k, 1)

                    def mean(at, tag, source, to):
                        mm(to[:, 0:T], mean_d[:], source, start=True, stop=True).then_inc(S[f"{tag}_mean"], 1)

                    def variance(at, tag, source, to, over=mean_d):
                        pe.wait_ge(S[f"{tag}_sq"], at(f"{tag}_sq"))
                        for j, s in enumerate(source):
                            last = mm(to[:, T:2 * T], over[:], s, start=j == 0, stop=j == len(source) - 1)
                        last.then_inc(S[f"{tag}_var"], 1)

                    def broadcast(name, g, q, first):
                        for n in range(2):
                            last = mm(ring[q][:, n * T:(n + 1) * T], pick[:, first + g * U + 2 * q + n], bc[:], start=True, stop=True)
                        last.then_inc(S[name], 1)

                    def broadcast_b(g):
                        for q in range(2):
                            pe.wait_ge(S["hc"], now("hc", 2 * g - 1 + q if g else 0))
                            broadcast("Bb", g, q, 0)

                    def broadcast_c(g):
                        for q in range(2):
                            pe.wait_ge(S["Bused"], now("Bused", 2 * g + q + 1))
                            broadcast("Cb", g, q, NS)

                    def sum_states(g):
                        hv = H[g % 2][:].rearrange("p (j n) t -> p n j t", j=NH)
                        pe.wait_ge(S["hc"], now("hc", 2 * g + 2))
                        for n in range(U):
                            last = mm(yb[:], ident[:], hv[:, n], start=g == 0 and n == 0, stop=g == NU - 1 and n == U - 1)
                        last.then_inc(S["ysum"], 1)

                    def scores(first, last):
                        for f in range(first, last):
                            c, e, h = f // 8, f % 2, f // 2 % 4 * 2
                            pe.wait_ge(S["mx"], was("mx", f - 1 if f >= 2 else 0))
                            rows = slice(64 * e, 64 * e + KR)
                            for n in range(2):
                                ins = mm(sbank[f % 2][:, n * T:(n + 1) * T], stack[rows, 0, h + n, c * P:(c + 1) * P],
                                         stack[rows, 1, h + n, :], start=True, stop=True)
                            ins.then_inc(S["smax"], 1)

                    def transpose_maxima():
                        pe.wait_ge(S["mx"], was("mx", FILLS))
                        pe.wait_ge(S["vc"], was("vc"))
                        for c in range(NC):
                            last = nc.tensor.transpose(qb[0:NHD, c * P:(c + 1) * P], mx[:, c], ident[:])
                        last.then_inc(S["mxT"], 1)

                    def weigh(h):
                        pe.wait_ge(S["pt"], was("pt", h + 1))
                        for c in range(NC):
                            to = fb[:, (c * NHD + h) * V1:(c * NHD + h + 1) * V1]
                            for m in range(NC):
                                last = mm(to, PT[:, h % RD, m, c * P:(c + 1) * P], vA[:, m, h], start=m == 0, stop=m == NC - 1)
                        if h == NHD - 1:
                            last.then_inc(S["pv"], 1)

                    def weighed(first, last):
                        for h in range(first, last):
                            e, n = h % 2, h // 2
                            pe.wait_ge(S["pt"], was("pt", h - 1 if h >= 2 else 0))
                            rows = slice(64 * e, 64 * e + KR + 3)
                            for c in range(NC):
                                ins = mm(sbank[h % 2][:, c * T:(c + 1) * T], stack[rows, 1, n, c * P:(c + 1) * P], stack[rows, 0, n, :], start=True, stop=True)
                            ins.then_inc(S["st"], 1)
                            if h >= 1:
                                weigh(h - 1)
                        if last == NHD:
                            weigh(NHD - 1)

                    if scan:
                        broadcast_b(0)
                    if att:
                        pe.wait_ge(s_stack, 16 * 24 * k)
                        pe.wait_ge(S["pt"], was("pt", 0))
                        scores(0, 4)
                    if scan:
                        broadcast_c(0)
                    if att:
                        scores(4, 10)
                    if scan:
                        broadcast_b(1)
                        sum_states(0)
                        broadcast_c(1)
                    if att:
                        scores(10, 16)
                        transpose_maxima()
                    if scan:
                        broadcast_b(2)
                        sum_states(1)
                        broadcast_c(2)
                    if att:
                        pe.wait_ge(s_mrow, 16 * 6 * k)
                        weighed(0, 8)
                    if scan:
                        broadcast_b(3)
                        sum_states(2)
                        broadcast_c(3)
                    if prep:
                        mean(then, "ln1", token_block(x_all, k, 1), pb)
                    if att:
                        weighed(8, 16)
                    if scan:
                        sum_states(3)
                    if att:
                        pe.wait_ge(S["yn"], was("yn"))
                        for c in range(NC):
                            last = nc.tensor.transpose(fb[:, c * P:(c + 1) * P], yn[:, c], ident[:])
                        last.then_inc(S["ynT"], 1)
                    if prep:
                        variance(then, "ln1", [psq[:]], pb)
                    if scan:
                        variance(now, "rms", [qsq[:, j] for j in range(NH)], yb, mean_i)
                    if att:
                        pe.wait_ge(S["ynTc"], was("ynTc"))
                        mm(fb[:, 0:T], w_proj[:], ynT[:], start=True, stop=True).then_inc(S["proj"], 1)
                    if prep:
                        pe.wait_ge(S["h1"], then("h1"))
                        for j in range(NH):
                            last = mm(pb[:, j * T:(j + 1) * T], w_inT[:, j * P:(j + 1) * P], h1[:], start=True, stop=True)
                        last.then_inc(S["xz_x"], 1)
                    if scan:
                        pe.wait_ge(S["yout"], now("yout"))
                        for j in range(NH):
                            last = mm(yb[:, 0:T], w_outT[:, j], y_s[:, j], start=j == 0, stop=j == NH - 1)
                        last.then_inc(S["mix"], 1)
                    if att:
                        pe.wait_ge(S["x2"], was("x2"))
                        mean(was, "mo", x2[:], fb)
                    if prep:
                        pe.wait_ge(S["xp"], then("xp"))
                        for j in range(NH):
                            last = mm(pb[:, j * T:(j + 1) * T], w_inT[:, (NH + j) * P:(NH + j + 1) * P], h1[:], start=True, stop=True)
                        last.then_inc(S["xz_z"], 1)
                    if scan:
                        pe.wait_ge(S["x1"], now("x1"))
                        mean(now, "ln2", x1[:], yb)
                    if att:
                        variance(was, "mo", [fsq[:]], fb)
                    if scan:
                        variance(now, "ln2", [qsq[:, 0]], yb)
                        pe.wait_ge(S["h2"], now("h2"))
                        mean(now, "at", h2[:], yb)
                    if prep:
                        pe.wait_ge(S["silu"], then("silu"))
                        for j in range(NH):
                            mm(pb[0:96, 0:T], w_dbl[:, j], sil[:, j], start=j == 0, stop=j == NH - 1)
                        for j in range(NH):
                            last = mm(pb[0:R, T:2 * T], w_rank[:, j], sil[:, j], start=j == 0, stop=j == NH - 1)
                        last.then_inc(S["dbl"], 1)
                    if scan:
                        variance(now, "at", [qsq[:, 1]], yb)
                    if prep:
                        pe.wait_ge(S["bc"], then("bc"))
                        for j in range(NH):
                            last = mm(pb[:, j * T:(j + 1) * T], w_dtT[:, j * P:(j + 1) * P], rank_s[:], start=True, stop=True)
                        last.then_inc(S["dtp"], 1)
                    if scan:
                        pe.wait_ge(S["hn"], now("hn"))
                        for n, w in enumerate((w_q, w_k)):
                            last = mm(qb[:, n * T:(n + 1) * T], w[:], hn[:], start=True, stop=True)
                        last.then_inc(S["qk"], 1)
                        pe.wait_ge(S["r1"], now("r1"))
                        for c in range(NC):
                            last = mm(qb[:, c * D:(c + 1) * D], hn[:, c * P:(c + 1) * P], w_v[:], start=True, stop=True)
                        last.then_inc(S["v"], 1)
                pipeline(pe, turn)

        with nc.Block() as block:
            @block.sync
            def _(sp):
                with sp.Fori(0, B) as i:
                    now = counts(sp, i)
                    sp.wait_ge(S["m_out"], now("m_out"))
                    sp.dma_start(out[bass.ds(i, 1)].rearrange("a d t -> (a d) t"), ot[0]).then_inc(s_store, 16)
                sp.wait_ge(s_store, 16 * B + 16)

            @block.gpsimd
            def _(pool):
                with pool.Fori(0, B) as i:
                    now = counts(pool, i)
                    pool.wait_ge(S["m_xm"], now("m_xm", 0))
                    nc.gpsimd.tensor_copy(xfc, xf_all[:, bass.ds(i, 1), :].rearrange("p a t -> p (a t)")).then_inc(S["m_x"], 1)

            @block.scalar
            def _(act):
                with act.Fori(0, B) as i:
                    now = counts(act, i)
                    for f in range(NP_):
                        act.wait_ge(S["m_up"], now("m_up", f + 1))
                        nc.scalar.activation(gel[f % 4], banks[f % 4][:].rearrange("p (c t) -> p c t", t=T),
                                             ACT.Gelu_apprx_tanh, bias=zero[:]).then_inc(S["m_gel"], 1)

            @block.vector
            def _(dve):
                with dve.Fori(0, B) as i:
                    now = counts(dve, i)
                    link = chained(dve, now, "m_chv")
                    dve.wait_ge(S["m_lg"], now("m_lg"))
                    link(nc.vector.tensor_copy(lg[:], fb[:, 0:NC * E].rearrange("p (c e) -> p c e", e=E)))
                    link(nc.vector.tensor_reduce(top[:, 0], lg[:], AX.X, ALU.max))
                    for c in range(NC):
                        last = nc.vector.scalar_tensor_tensor(key[:, c], lg[:, c], top[:, 0, c:c + 1], rank_e[:], ALU.is_equal, ALU.mult)
                    link(last)
                    link(nc.vector.tensor_reduce(top[:, 1], key[:], AX.X, ALU.max))
                    for c in range(NC):
                        last = nc.vector.tensor_scalar(hot[:, c], key[:, c], top[:, 1, c:c + 1], None, ALU.is_equal)
                    last.then_inc(S["m_hot"], 1)
                    for k in range(E // 2):
                        dve.wait_ge(S["m_mask"], now("m_mask", k + 1))
                        nc.vector.tensor_tensor(xm[:, 2 * k:2 * k + 2], xfc.rearrange("p (a t) -> p a t", a=1).to_broadcast([P, 2, T]),
                                                sbank[k % 2][:].rearrange("p (e t) -> p e t", t=T), ALU.mult).then_inc(S["m_xm"], 1)
                    dve.wait_ge(S["m_y"], now("m_y"))
                    link(nc.vector.tensor_copy(gb_f[:], column(mods, 5, 1, i)))
                    dve.wait_ge(s_store, i * 16 + 16)
                    nc.vector.scalar_tensor_tensor(ot[0], yb[:, 0:T], gb_f[:], x_all[:, bass.ds(i, 1), :].rearrange("p a t -> p (a t)"), ALU.mult, ALU.add).then_inc(S["m_out"], 1)
                    link.close()

            @block.tensor
            def _(pe):
                with pe.Fori(0, B) as i:
                    now = counts(pe, i)
                    mm = nc.tensor.matmul
                    pe.wait_ge(S["m_x"], now("m_x"))
                    for c in range(NC):
                        mm(fb[:, c * E:(c + 1) * E], xfc[:, c * P:(c + 1) * P], gate_w[:], start=True, stop=False)
                        last = mm(fb[:, c * E:(c + 1) * E], ones_row[:], gate_b[:], start=False, stop=True)
                    last.then_inc(S["m_lg"], 1)
                    pe.wait_ge(S["m_hot"], now("m_hot"))
                    pe.wait_ge(S["m_gel"], now("m_gel", 0))
                    for k in range(E // 2):
                        if k >= 2:
                            pe.wait_ge(S["m_xm"], now("m_xm", k - 1))
                        for e in range(2):
                            for c in range(NC):
                                last = mm(sbank[k % 2][:, e * T + c * P:e * T + (c + 1) * P],
                                          hot[:, c, 2 * k + e:2 * k + e + 1].to_broadcast([P, P]), ident_b[:], start=True, stop=True)
                        last.then_inc(S["m_mask"], 1)
                    pe.wait_ge(S["m_out"], now("m_out", 0))

                    def down(f):
                        pe.wait_ge(S["m_gel"], now("m_gel", f + 1))
                        for c in range(2):
                            h = 2 * f + c
                            last = mm(yb[:, 0:T], w2[:, h // HC, h % HC], gel[f % 4][:, c], start=h == 0, stop=h == E * HC - 1)
                        if f == NP_ - 1:
                            last.then_inc(S["m_y"], 1)

                    pe.wait_ge(S["m_xm"], now("m_xm", E // 2))
                    for f in range(NP_):
                        if f >= 4:
                            pe.wait_ge(S["m_gel"], now("m_gel", f - 3))
                        for c in range(2):
                            h = 2 * f + c
                            last = mm(banks[f % 4][:, c * T:(c + 1) * T], w1[:, h // HC, (h % HC) * P:(h % HC + 1) * P], xm[:, h // HC], start=True, stop=True)
                        last.then_inc(S["m_up"], 1)
                        if f >= 2:
                            down(f - 2)
                    down(NP_ - 2)
                    down(NP_ - 1)


def kernel(**inputs):
    import numpy as np
    import concourse.bacc as bacc
    from concourse import mybir as mb
    from concourse.bass_utils import run_bass_kernel_spmd as run

    a = {k: np.asarray(v) for k, v in inputs.items()}
    P, DK = 128, 8

    def halves(v):
        return v.reshape((2, P) + v.shape[1:]).swapaxes(0, 1)

    w_xT = a["L0_attn_W_x"].T
    rank = a["L0_attn_W_dt"].shape[1]
    bc_cols = w_xT[:, rank:]

    def tiled_heads(w):
        return w.reshape(w.shape[0], -1, 2, DK).transpose(0, 2, 3, 1).reshape(w.shape[0], -1)

    qkv = a["L0_ffn_w_qkv"]
    D = qkv.shape[0]
    data = {
        "x": a["L0_attn_x"].transpose(0, 2, 1),
        "w_inT": a["L0_attn_W_in"].T,
        "w_conv": halves(a["L0_attn_W_conv"]),
        "b_conv": halves(a["L0_attn_b_conv"]),
        "w_dbl": halves(np.concatenate([bc_cols, bc_cols, bc_cols], axis=1)),
        "w_rank": halves(w_xT[:, :rank]),
        "w_dtT": a["L0_attn_W_dt"].T,
        "b_dt": halves(a["L0_attn_b_dt"]),
        "a_log": halves(a["L0_attn_A_log"]),
        "skip": halves(a["L0_attn_D"]),
        "rms_w": halves(a["L0_attn_rms_w"]),
        "w_outT": halves(a["L0_attn_W_out"].T),
        "ln": np.stack([a["L0_ffn_ln1_w"], a["L0_ffn_ln1_b"], a["L0_ffn_ln2_w"], a["L0_ffn_ln2_b"]], axis=1),
        "w_q": tiled_heads(qkv[:, :D]),
        "w_k": tiled_heads(qkv[:, D:2 * D]),
        "w_v": qkv[:, 2 * D:],
        "w_proj": a["L0_ffn_w_proj"],
        "gate_w": a["L0_ffn_gate_w"],
        "gate_b": a["L0_ffn_gate_b"][None],
        "w1": a["L0_ffn_w1"],
        "w2": a["L0_ffn_w2"],
        "cT": a["L0_c"].T,
        "w_mod": a["L0_wmod"].reshape(D, 6, D),
    }
    nc = bacc.Bacc("TRN2", target_bir_lowering=False, num_devices=1)
    arrays, io = {}, {}
    for name, v in data.items():
        v = np.ascontiguousarray(v)
        arrays[f"in_{name}"] = v
        io[name] = nc.dram_tensor(f"in_{name}", v.shape, mb.dt.from_np(v.dtype), kind="ExternalInput").ap()
    out = nc.dram_tensor("out_0", data["x"].shape, mb.dt.float32, kind="ExternalOutput").ap()
    adaln_block(nc, io, out)
    r = run(nc, [arrays], core_ids=[0])
    return np.ascontiguousarray(r.results[0]["out_0"].transpose(0, 2, 1))
```

```python
import concourse.bass as bass
from concourse import mybir
from contextlib import ExitStack
import math


def adaln_block(nc, io, out):
    fp32 = mybir.dt.float32
    bf16 = mybir.dt.bfloat16
    ALU = mybir.AluOpType
    ACT = mybir.ActivationFunctionType
    AX = mybir.AxisListType

    B, D, T = io["x"].shape
    P = 128
    NH = io["w_inT"].shape[1] // P // 2
    NS = io["a_log"].shape[2]
    TAPS = io["w_conv"].shape[2]
    R = io["w_dtT"].shape[0]
    DK = 8
    NHD = D // DK
    HS = NHD // 2
    E = io["gate_w"].shape[1]
    HC = io["w1"].shape[2] // P
    NC = T // P
    U = 4
    NU = NS // U
    ZU = NH * U
    FILLS = NHD
    SLOTS = [(0, 0), (0, 1), (0, 2), (1, 0), (1, 1), (2, 0)]
    KR = len(SLOTS) * DK
    VR = 32
    HPG = P // VR
    HG = NHD // HPG
    LEAST = -43.0
    RD = 3
    C = B * NC
    NT = (C + E) // 2 * 2
    FLOOR = math.exp(-10.0)
    assert B % 2 == 0 and D == P and NC * P == T and NC == 2 and NS % U == 0 and U == 4

    ctx = ExitStack()
    with ctx:
        def sb(name, shape, dt=fp32):
            return ctx.enter_context(nc.sbuf_tensor(name, shape, dt))

        per = {}
        S = {}

        def event(name, times=1):
            S[name] = ctx.enter_context(nc.semaphore(name))
            per[name] = times

        w_inT = sb("w_inT", [P, 2 * NH * P])
        w_conv = sb("w_conv", [P, NH, TAPS])
        b_conv = sb("b_conv", [P, NH])
        w_dbl = sb("w_dbl", [P, NH, 3 * 2 * NS + R])
        w_dtT = sb("w_dtT", [3 * 2 * NS + R, NH * P])
        b_dt = sb("b_dt", [P, NH])
        a_neg = sb("a_neg", [P, NH, NS])
        a_log = sb("a_log", [P, NH, NS])
        skip = sb("skip", [P, NH])
        rms_w = sb("rms_w", [P, NH])
        w_outT = sb("w_outT", [P, NH, D])
        ln = sb("ln", [P, 4])
        w_q = sb("w_q", [P, D])
        w_k = sb("w_k", [P, D])
        w_v = sb("w_v", [P, D])
        w_proj = sb("w_proj", [P, HG, D])
        spread = sb("spread", [P, P])
        gate_w = sb("gate_w", [P, E])
        gate_b = sb("gate_b", [1, E])
        w1 = sb("w1", [P, E, HC * P])
        w2 = sb("w2", [P, E, HC, D])
        cT = sb("cT", [P, B])
        c_tmp = sb("c_tmp", [P, 3, B])
        mods = sb("mods", [P, 6, B])
        mods_abs = sb("mods_abs", [P, 2, B])
        ident = sb("ident", [P, P])
        ident_b = sb("ident_b", [P, P], bf16)
        mean_d = sb("mean_d", [P, P])
        center_d = sb("center_d", [P, P])
        mean_i = sb("mean_i", [P, P])
        pick = sb("pick", [96, 2 * NS], bf16)
        ones_row = sb("ones_row", [1, P])
        eps_ln = sb("eps_ln", [P, 1])
        eps_rms = sb("eps_rms", [P, 1])
        one = sb("one", [P, 1])
        zero = sb("zero", [P, 1])
        rank_e = sb("rank_e", [P, E])

        x_all = sb("x_all", [P, B, T])
        xf_all = sb("xf_all", [P, B, T])

        mod_p = sb("mod_p", [P, 2])
        pcen = sb("pcen", [P, T])
        psq = sb("psq", [P, T])
        prs = sb("prs", [P, T])
        h1 = pcen
        xp = sb("xp", [P, NH, TAPS - 1 + T])
        pz = sb("pz", [P, 2 * NH, T])
        pm = sb("pm", [P, 2 * NH, T])
        sil = [sb(f"sil{k}", [P, 2 * NH, T]) for k in range(2)]
        rank_s = sb("rank_s", [3 * 2 * NS + R, T])
        bc_v = sb("bc_v", [96, T])
        bc = [sb(f"bc{k}", [96, T], bf16) for k in range(2)]
        sp_a, sp_r = pm[:, 0:NH], pm[:, NH:2 * NH]
        dt_s = [sb(f"dt_s{k}", [P, NH, T]) for k in range(2)]
        u_s = [sb(f"u_s{k}", [P, NH, T]) for k in range(2)]
        dA = [sb(f"dA{k}", [P, ZU, T]) for k in range(2)]
        H = [sb(f"H{k}", [P, ZU, T]) for k in range(2)]
        c_s = [sb(f"c_s{k}", [P, U, T]) for k in range(2)]
        part = sb("part", [P, NH, 2, T])
        y_sum = sb("y_sum", [P, NH, T])
        mod_q = sb("mod_q", [P, 3])
        y_s = sb("y_s", [P, NH, T])
        qsq = sb("qsq", [P, NH, T])
        qrs = sb("qrs", [P, T])
        qcen = sb("qcen", [P, T])
        hn = qcen
        qk_r = y_s
        qk_p = [sb(f"qk_p{k}", [P, 2, T], bf16) for k in range(3)]
        stack = [sb(f"stack{k}", [P, 2, HS, T], bf16) for k in range(2)]
        vA = [sb(f"vA{k}", [P, NC, NHD, VR]) for k in range(2)]
        mx = sb("mx", [P, NC, NHD])
        mx_r = sb("mx_r", [NHD, T])
        mx_p = sb("mx_p", [NHD, 3, T], bf16)
        PT = sb("PT", [P, RD, NC, T])
        w_mod = PT[:].rearrange("p r c t -> p (r c t)")[:, 0:6 * P].rearrange("p (m d) -> p m d", m=6)
        gb_f = sb("gb_f", [P, 1])
        o_s = sb("o_s", [P, HG, T])
        x2, fcen, fsq, frs = [o_s[:, g] for g in range(4)]
        xf = sb("xf", [P, T])
        lg_all = sb("lg_all", [P, B, NC * E])
        ones_b = sb("ones_b", [P, P], bf16)
        before = sb("before", [P, P], bf16)
        hot_b = sb("hot_b", [P, C * E], bf16)
        place = sb("place", [P, C], mybir.dt.uint32)
        expert_i = sb("expert_i", [P, NT], mybir.dt.int32)
        sorted_x = nc.dram_tensor("sorted_x", [NT * P, D], fp32, kind="Internal").ap()
        sorted_y = nc.dram_tensor("sorted_y", [NT * P, D], fp32, kind="Internal").ap()

        def bank(k):
            return ctx.enter_context(nc.psum_tensor(f"bank{k}", [P, 512], fp32))

        pb, ring0, ring1, wb, qb, f0, f1, s0 = [bank(k) for k in range(8)]
        ring = [ring0, ring1]
        fb = [f0, f1]

        CONSTS = 5
        s_load = ctx.enter_context(nc.semaphore("s_load"))
        s_late = ctx.enter_context(nc.semaphore("s_late"))
        s_const = ctx.enter_context(nc.semaphore("s_const"))
        s_mod = ctx.enter_context(nc.semaphore("s_mod"))
        s_silc = ctx.enter_context(nc.semaphore("s_silc"))
        s_setup = ctx.enter_context(nc.semaphore("s_setup"))

        loads = [(x_all[:], io["x"].rearrange("b d t -> d b t")), (w_inT[:], io["w_inT"]), (w_conv[:], io["w_conv"]),
                 (b_conv[:], io["b_conv"]), (w_dbl[:], io["w_dbl"]), (w_dtT[96:96 + R], io["w_dtT"]),
                 (b_dt[:], io["b_dt"]), (a_log[:], io["a_log"]), (skip[:], io["skip"]), (rms_w[:], io["rms_w"]),
                 (w_outT[:], io["w_outT"]), (ln[:], io["ln"]), (w_q[:], io["w_q"]), (w_k[:], io["w_k"]), (w_v[:], io["w_v"]),
                 (gate_w[:], io["gate_w"]), (gate_b[:], io["gate_b"]), (cT[:], io["cT"]),
                 (w_mod, io["w_mod"])]
        head_loads = []
        for j in range(HPG):
            head_loads.append((w_proj[VR * j:VR * j + DK], io["w_proj"].rearrange("(g j v) d -> j v g d", j=HPG, v=DK)[j]))
        late_loads = [(w1[:], io["w1"].rearrange("e d h -> d e h")), (w2[:], io["w2"].rearrange("e (c p) d -> p e c d", p=P))]

        len_zeros = 5 * T
        zeros = xf_all[:, B - 5:B].rearrange("p b t -> p (b t)")
        LATE = 16 * (len(head_loads) + len(late_loads) + NT * D // len_zeros)
        assert NT * D % len_zeros == 0

        with nc.Block() as block:
            @block.sync
            def _(sp):
                for tile, src in loads:
                    sp.dma_start(tile, src).then_inc(s_load, 16)
                sp.wait_ge(s_const, 1)
                for tile, src in head_loads:
                    sp.dma_start(tile, src).then_inc(s_late, 16)
                for tile, src in late_loads:
                    sp.dma_start(tile, src).then_inc(s_late, 16)
                rows = sorted_x.rearrange("(p r) d -> p (r d)", p=P)
                for k in range(0, NT * D, len_zeros):
                    sp.dma_start(rows[:, k:k + len_zeros], zeros).then_inc(s_late, 16)
                sp.wait_ge(s_load, 16 * len(loads))

            @block.gpsimd
            def _(pool):
                nc.gpsimd.memset(zeros, 0.0)
                nc.gpsimd.memset(w_proj[:], 0.0)
                nc.gpsimd.memset(spread[:], 1.0)
                nc.gpsimd.memset(ident[:], 0.0)
                nc.gpsimd.memset(mean_d[:], 1.0 / D)
                nc.gpsimd.memset(mean_i[:], 1.0 / (NH * P))
                nc.gpsimd.memset(pick[:], 0.0)
                nc.gpsimd.memset(ones_row[:], 1.0)
                nc.gpsimd.memset(eps_ln[:], 1e-5)
                nc.gpsimd.memset(eps_rms[:], 1e-6)
                nc.gpsimd.memset(one[:], 1.0)
                nc.gpsimd.memset(zero[:], 0.0)
                nc.gpsimd.memset(stack[0][:, 1], -1.0)
                nc.gpsimd.memset(stack[1][:, 1], -1.0).then_inc(s_const, 1)
                pool.wait_ge(s_const, 1)
                nc.gpsimd.affine_select(out=ident[:], in_=ident[:], compare_op=ALU.not_equal, fill=1.0, base=0,
                                        pattern=[[-1, P]], channel_multiplier=1)
                count = 1
                for part in range(3):
                    nc.gpsimd.affine_select(out=pick[:], in_=pick[:], compare_op=ALU.not_equal, fill=1.0,
                                            base=-2 * NS * part, pattern=[[-1, 2 * NS]],
                                            channel_multiplier=1).then_inc(s_const, 1)
                    count += 1
                    pool.wait_ge(s_const, count)
                nc.gpsimd.affine_select(out=spread[:], in_=spread[:], compare_op=ALU.is_equal, fill=0.0, base=-DK,
                                        pattern=[[-VR, HPG], [0, VR]], channel_multiplier=1)
                nc.gpsimd.iota(rank_e[:], pattern=[[-1, E]], base=E, channel_multiplier=0,
                               allow_small_or_imprecise_dtypes=True)
                nc.gpsimd.tensor_tensor(center_d[:], ident[:], mean_d[:], ALU.subtract)
                nc.gpsimd.tensor_copy(ident_b[:], ident[:]).then_inc(s_const, 1)
                assert count + 1 == CONSTS

            @block.scalar
            def _(act):
                nc.scalar.preload_act_table_set("natural_log_exp_and_others")
                act.wait_ge(s_load, 16 * len(loads))
                act.wait_ge(s_const, CONSTS)
                nc.scalar.activation(a_neg[:], a_log[:], ACT.Exp, bias=zero[:]).then_inc(s_silc, 1)
                act.wait_ge(s_mod, 1)
                nc.scalar.activation(c_tmp[:, 1], c_tmp[:, 0], ACT.Exp, bias=zero[:], scale=-1.0).then_inc(s_silc, 1)
                act.wait_ge(s_silc, 2)
                nc.scalar.activation(c_tmp[:, 2], c_tmp[:, 1], ACT.Ln, bias=one[:]).then_inc(s_silc, 1)
                act.wait_ge(s_silc, 3)
                nc.scalar.activation(c_tmp[:, 1], c_tmp[:, 2], ACT.Exp, bias=zero[:], scale=-1.0).then_inc(s_silc, 1)

            @block.vector
            def _(dve):
                count = 0

                def link(ins):
                    nonlocal count
                    count += 1
                    ins.then_inc(s_mod, 1)
                    dve.wait_ge(s_mod, count)

                dve.wait_ge(s_load, 16 * len(loads))
                link(nc.vector.tensor_scalar(c_tmp[:, 0], cT[:], LEAST, None, ALU.max))
                nc.vector.memset(xp[:, :, 0:TAPS - 1], 0.0)
                for k in range(2):
                    nc.vector.memset(vA[k][:, :, :, DK:VR], 1.0)
                for k in range(2):
                    nc.vector.memset(dA[k][:, :, 0:1], 0.0)
                dve.wait_ge(s_silc, 1)
                nc.vector.tensor_scalar(a_neg[:], a_neg[:], -1.0, None, ALU.mult)
                dve.wait_ge(s_silc, 4)
                link(nc.vector.tensor_tensor(c_tmp[:, 0], cT[:], c_tmp[:, 1], ALU.mult))
                dve.wait_ge(s_setup, 1)
                link(nc.vector.tensor_copy(mods[:], wb[:, 0:6 * B].rearrange("p (m b) -> p m b", b=B)))
                for m in (1, 4):
                    nc.vector.tensor_scalar(mods[:, m], mods[:, m], 1.0, None, ALU.add)
                for k, m in enumerate((2, 5)):
                    link(nc.vector.tensor_scalar(c_tmp[:, 1], mods[:, m], -1.0, None, ALU.mult))
                    link(nc.vector.tensor_tensor(mods_abs[:, k], mods[:, m], c_tmp[:, 1], ALU.max))
                    link(nc.vector.tensor_scalar(mods_abs[:, k], mods_abs[:, k], 0.25, None, ALU.max))
                    link(nc.vector.tensor_scalar(c_tmp[:, 2], mods[:, m], 0.0, 2.0, ALU.is_ge, ALU.mult))
                    link(nc.vector.tensor_scalar(c_tmp[:, 2], c_tmp[:, 2], -1.0, None, ALU.add))
                    link(nc.vector.tensor_tensor(mods[:, m], c_tmp[:, 2], mods_abs[:, k], ALU.mult))

            @block.tensor
            def _(pe):
                pe.wait_ge(s_mod, 2)
                for m in range(6):
                    last = nc.tensor.matmul(wb[:, m * B:(m + 1) * B], w_mod[:, m], c_tmp[:, 0],
                                            start=True, stop=True)
                last.then_inc(s_setup, 1)

        for tag in ("ln1", "rms", "ln2", "at", "mo"):
            for step in ("cen", "sq", "var", "rs"):
                event(f"{tag}_{step}")
        for name, times in (
                ("h1", 1), ("xz_x", 1), ("xp", 1), ("xz_z", 1), ("tap0", 1), ("z", 1), ("cut", 1), ("sig_a", 1),
                ("sig_b", 1), ("sig", 1), ("silu", 1), ("dbl", 1), ("rank", 1), ("bc", 1), ("dtp", 1),
                ("softp_a", 1), ("softp_b", 1), ("softp", 1), ("dt", 1), ("u", 1),
                ("dec", 2 * NU), ("clamp", NU), ("Bb", 2 * NU), ("Bused", 2 * NU), ("Cb", 2 * NU), ("Cc", 2 * NU),
                ("scan", NU), ("hc", 2 * NU), ("sum", NU),
                ("yraw", 1), ("rms_add", 1), ("yout", 1), ("mix", 1), ("x1", 1), ("h2", 1), ("hn", 1), ("qk", 1), ("hi", 1),
                ("r1", 1), ("mid", 1), ("lo", 1), ("v", 1), ("vc", 1),
                ("smax", FILLS), ("mx", FILLS), ("mxT", 1), ("mxp", 1),
                ("st", FILLS), ("pt", FILLS), ("pv", 2), ("vs", 2), ("den", 2), ("inv", 2), ("div", 2),
                ("proj", 1), ("x2", 1), ("fin", 1), ("xf", 1), ("tok", 1), ("tokc", 1),
                ("act_p", 1), ("act_q", 3), ("act_f", 3), ("dve_p", 9), ("dve_q", 3), ("dve_m", 3), ("dve_f", 2),
                ("pool_s", 4)):
            event(name, times)
        s_stack = ctx.enter_context(nc.semaphore("s_stack"))
        s_mrow = ctx.enter_context(nc.semaphore("s_mrow"))
        for name in ("e_turned", "e_xt", "e_up", "e_gelu", "e_ht", "e_htc", "e_down", "e_y",
                     "f_turned", "f_gate", "f_out"):
            event(name)

        def start_counts(sp):
            for name in per:
                sp.sem_inc(S[name], 2)

        kept = {}

        def times(eng, turn, n):
            if isinstance(turn, int) or n == 1:
                return turn * n if isinstance(turn, int) else turn
            known = kept.setdefault((id(eng), id(turn)), (turn, {}))[1]
            if n not in known:
                known[n] = eng.snap(turn * n)
            return known[n]

        def counts(eng, turn, shift=0):
            def count(name, k=1):
                return times(eng, turn, per[name]) + (shift * per[name] + k + 2)
            return count

        def chained(eng, at, name):
            count = 0

            def link(ins):
                nonlocal count
                count += 1
                assert count <= per[name]
                ins.then_inc(S[name], 1)
                eng.wait_ge(S[name], at(name, count))

            def close():
                assert count == per[name], (name, count)
            link.close = close
            return link

        def pipeline(eng, turn):
            def peeled(k):
                turn(k, 0, k % 2, prep=k + 1 < B, scan=0 <= k < B, query=0 <= k - 1 < B, maxi=0 <= k - 2 < B,
                     weigh=0 <= k - 3 < B)
            for k in range(-1, 3):
                peeled(k)
            with eng.Fori(3, B - 2, 2) as k:
                turn(k, 0, 1, True, True, True, True, True)
                turn(k, 1, 0, True, True, True, True, True)
            for k in range(B - 1, B + 3):
                peeled(k)

        def token_block(t, k, shift=0):
            return t[:, bass.ds(k + shift, 1), :].rearrange("p a t -> p (a t)")

        def column(t, m, n, k, shift=0):
            return t[:, m:m + n, bass.ds(k + shift, 1)].rearrange("p m a -> p (m a)")

        with nc.Block() as block:
            @block.sync
            def _(sp):
                start_counts(sp)

        with nc.Block() as block:
            @block.sync
            def _(sp):
                def turn(k, d, p, prep, scan, query, maxi, weigh):
                    at_q, at_m = counts(sp, k, d - 1), counts(sp, k, d - 2)
                    if query:
                        sp.wait_ge(S["lo"], at_q("lo"))
                        for qk in range(2):
                            for slot, parts in enumerate(SLOTS):
                                for e in range(2):
                                    row = 64 * e + slot * DK
                                    sp.dma_start(stack[1 - p][row:row + DK, qk],
                                                 qk_p[parts[qk]][64 * e:64 * e + DK * HS, qk]).then_inc(s_stack, 16)
                    if maxi:
                        sp.wait_ge(S["mxp"], at_m("mxp"))
                        for e in range(2):
                            for part in range(3):
                                row = 64 * e + KR + part
                                sp.dma_start(stack[p][row:row + 1, 0], mx_p[e * HS:(e + 1) * HS, part]).then_inc(s_mrow, 16)
                pipeline(sp, turn)

            @block.gpsimd
            def _(pool):
                Hv = [t[:].rearrange("p (j n) t -> p j n t", j=NH) for t in H]
                tt = nc.gpsimd.tensor_tensor

                def turn(k, d, p, prep, scan, query, maxi, weigh):
                    now, then, at_q = counts(pool, k, d), counts(pool, k, d + 1), counts(pool, k, d - 1)
                    link = chained(pool, now, "pool_s")

                    def outputs(g, q):
                        pool.wait_ge(S["scan"], now("scan", g + 1))
                        pool.wait_ge(S["Cc"], now("Cc", 2 * g + q + 1))
                        h = Hv[g % 2][:, :, 2 * q:2 * q + 2]
                        c = c_s[g % 2][:, 2 * q:2 * q + 2].rearrange("p (a n) t -> p a n t", a=1)
                        tt(h, h, c.to_broadcast([P, NH, 2, T]), ALU.mult).then_inc(S["hc"], 1)

                    def sum_states(g):
                        h = Hv[g % 2]
                        pool.wait_ge(S["hc"], now("hc", 2 * g + 2))
                        if g == 0:
                            tt(part[:], h[:, :, 0:2], h[:, :, 2:4], ALU.add).then_inc(S["sum"], 1)
                            return
                        link(tt(h[:, :, 0:2], h[:, :, 0:2], h[:, :, 2:4], ALU.add))
                        if g < NU - 1:
                            pool.wait_ge(S["sum"], now("sum", g))
                            tt(part[:], part[:], h[:, :, 0:2], ALU.add).then_inc(S["sum"], 1)
                        else:
                            link(tt(part[:], part[:], h[:, :, 0:2], ALU.add))
                            if query:
                                pool.wait_ge(S["yraw"], at_q("yraw"))
                            tt(y_sum[:], part[:, :, 0], part[:, :, 1], ALU.add).then_inc(S["sum"], 1)

                    if query:
                        pool.wait_ge(S["yraw"], at_q("yraw"))
                        tt(y_s[:], y_s[:], sil[1 - p][:, NH:], ALU.mult).then_inc(S["rms_cen"], 1)
                        pool.wait_ge(S["rms_sq"], at_q("rms_sq"))
                        tt(qsq[:, 0], qsq[:, 0], qsq[:, 1], ALU.add).then_inc(S["rms_add"], 1)
                    if scan:
                        outputs(0, 0)
                        outputs(0, 1)
                        sum_states(0)
                        outputs(1, 0)
                        outputs(1, 1)
                        sum_states(1)
                    if prep:
                        pool.wait_ge(S["sig"], then("sig"))
                        tt(sil[1 - p][:], pz[:], pm[:], ALU.mult).then_inc(S["silu"], 1)
                    if scan:
                        outputs(2, 0)
                        outputs(2, 1)
                        sum_states(2)
                        outputs(3, 0)
                    if prep:
                        pool.wait_ge(S["dt"], then("dt"))
                        tt(u_s[1 - p][:], dt_s[1 - p][:], sil[1 - p][:, 0:NH], ALU.mult).then_inc(S["u"], 1)
                    if scan:
                        outputs(3, 1)
                        sum_states(3)
                    if scan:
                        link.close()
                pipeline(pool, turn)

            @block.scalar
            def _(act):
                nc.scalar.preload_act_table_set("natural_log_exp_and_others")
                two = "p (a t) -> p a t"

                def turn(k, d, p, prep, scan, query, maxi, weigh):
                    now, then = counts(act, k, d), counts(act, k, d + 1)
                    at_q, at_w = counts(act, k, d - 1), counts(act, k, d - 3)
                    stacked = times(act, k, 16 * 24) + (d - 1) * (16 * 24)
                    link_p, link_q, link_f = chained(act, then, "act_p"), chained(act, at_q, "act_q"), chained(act, at_w, "act_f")

                    def square(at, tag, source, result):
                        act.wait_ge(S[f"{tag}_cen"], at(f"{tag}_cen"))
                        nc.scalar.activation(result, source, ACT.Square, bias=zero[:]).then_inc(S[f"{tag}_sq"], 1)

                    def inverse_root(at, link, tag, variance, eps, result):
                        act.wait_ge(S[f"{tag}_var"], at(f"{tag}_var"))
                        link(nc.scalar.activation(result, variance, ACT.Ln, bias=eps))
                        nc.scalar.activation(result, result, ACT.Exp, bias=zero[:], scale=-0.5).then_inc(S[f"{tag}_rs"], 1)

                    def weights(first, last):
                        for f in range(first, last):
                            act.wait_ge(S["st"], at_w("st", f + 1))
                            nc.scalar.activation(PT[:, f % RD], wb[:].rearrange(two, t=T), ACT.Exp,
                                                 bias=zero[:], scale=float(DK) ** -0.5).then_inc(S["pt"], 1)

                    def decay(g, j):
                        mine, unit, dt_u = (now, g + 2, dt_s[p]) if g + 2 < NU else (then, g + 2 - NU, dt_s[1 - p])
                        if j == 0:
                            act.wait_ge(S["dt"], mine("dt"))
                            if scan:
                                act.wait_ge(S["scan"], now("scan", g + 1))
                        for n in range(U):
                            last = nc.scalar.activation(dA[g % 2][:, j * U + n, 1:T], dt_u[:, j, 1:T], ACT.Exp, bias=zero[:],
                                                        scale=a_neg[:, j, unit * U + n:unit * U + n + 1])
                        last.then_inc(S["dec"], 1)

                    def keep_values(n):
                        act.wait_ge(S["pv"], at_w("pv", n + 1))
                        nc.scalar.activation(o_s[:, 2 * n:2 * n + 2], fb[n][:].rearrange(two, t=T), ACT.Copy).then_inc(S["vs"], 1)

                    def inverse_sums(n):
                        act.wait_ge(S["den"], at_w("den", n + 1))
                        link_f(nc.scalar.activation(fb[n][:], fb[n][:], ACT.Ln, bias=zero[:]))
                        nc.scalar.activation(fb[n][:], fb[n][:], ACT.Exp, bias=zero[:], scale=-1.0).then_inc(S["inv"], 1)

                    def keep_c(g, q):
                        if g >= 2:
                            act.wait_ge(S["hc"], now("hc", 2 * (g - 2) + q + 1))
                        elif query:
                            act.wait_ge(S["hc"], at_q("hc", 2 * (g + 2) + q + 1))
                        act.wait_ge(S["Cb"], now("Cb", 2 * g + q + 1))
                        nc.scalar.activation(c_s[g % 2][:, 2 * q:2 * q + 2], ring[q][:].rearrange(two, t=T), ACT.Copy).then_inc(S["Cc"], 1)

                    if prep:
                        square(then, "ln1", pb[:, 0:T], psq[:])
                        inverse_root(then, link_p, "ln1", pb[:, T:2 * T], eps_ln[:], prs[:])
                    if query:
                        square(at_q, "rms", y_s[:], qsq[:])
                    if scan:
                        keep_c(0, 0)
                    if query:
                        inverse_root(at_q, link_q, "rms", qb[:, T:2 * T], eps_rms[:], qrs[:])
                    if scan:
                        keep_c(0, 1)
                    if prep:
                        act.wait_ge(S["xz_x"], then("xz_x"))
                        nc.scalar.activation(xp[:, :, TAPS - 1:], pb[:].rearrange(two, t=T), ACT.Copy).then_inc(S["xp"], 1)
                    if weigh:
                        weights(0, 1)
                    if scan:
                        decay(0, 0)
                    if weigh:
                        weights(1, 2)
                    if prep:
                        act.wait_ge(S["xp"], then("xp"))
                        for j in range(NH):
                            last = nc.scalar.activation(pz[:, j], xp[:, j, 0:T], ACT.Identity, bias=b_conv[:, j:j + 1], scale=w_conv[:, j, 0:1])
                        last.then_inc(S["tap0"], 1)
                    if weigh:
                        weights(2, 3)
                    if prep:
                        act.wait_ge(S["xz_z"], then("xz_z"))
                        nc.scalar.activation(pz[:, NH:2 * NH], pb[:].rearrange(two, t=T), ACT.Copy).then_inc(S["z"], 1)
                    if scan:
                        keep_c(1, 0)
                    if weigh:
                        weights(3, 4)
                    if scan:
                        decay(0, 1)
                    if weigh:
                        weights(4, 5)
                    if query:
                        square(at_q, "ln2", qb[:, 0:T], qsq[:, 0])
                    if scan:
                        keep_c(1, 1)
                    if weigh:
                        weights(5, 6)
                    if prep:
                        act.wait_ge(S["cut"], then("cut"))
                        nc.scalar.activation(pm[:], pm[:], ACT.Exp, bias=zero[:], scale=-1.0).then_inc(S["sig_a"], 1)
                    if weigh:
                        weights(6, 7)
                    if query:
                        inverse_root(at_q, link_q, "ln2", qb[:, T:2 * T], eps_ln[:], qrs[:])
                    if weigh:
                        weights(7, 8)
                    if prep:
                        act.wait_ge(S["sig_a"], then("sig_a"))
                        nc.scalar.activation(pm[:], pm[:], ACT.Ln, bias=one[:]).then_inc(S["sig_b"], 1)
                    if weigh:
                        weights(8, 9)
                    if prep:
                        act.wait_ge(S["sig_b"], then("sig_b"))
                        nc.scalar.activation(pm[:], pm[:], ACT.Exp, bias=zero[:], scale=-1.0).then_inc(S["sig"], 1)
                    if query:
                        square(at_q, "at", qb[:, 0:T], qsq[:, 1])
                    if weigh:
                        weights(9, 10)
                    if scan:
                        decay(1, 0)
                    if weigh:
                        weights(10, 11)
                    if query:
                        inverse_root(at_q, link_q, "at", qb[:, T:2 * T], eps_ln[:], qrs[:])
                    if weigh:
                        weights(11, 12)
                    if scan:
                        decay(1, 1)
                    if weigh:
                        weights(12, 13)
                    if prep:
                        act.wait_ge(S["dbl"], then("dbl"))
                        nc.scalar.activation(rank_s[96:96 + R], pb[96:96 + R, 0:T], ACT.Copy).then_inc(S["rank"], 1)
                    if scan:
                        keep_c(2, 0)
                    if weigh:
                        weights(13, 14)
                    if scan:
                        keep_c(2, 1)
                    if weigh:
                        keep_values(0)
                        weights(14, 15)
                        inverse_sums(0)
                        weights(15, 16)
                    if query:
                        if maxi:
                            act.wait_ge(s_stack, stacked)
                        act.wait_ge(S["qk"], at_q("qk"))
                        nc.scalar.activation(qk_p[0][:], qb[:].rearrange(two, t=T), ACT.Copy).then_inc(S["hi"], 1)
                    if prep:
                        act.wait_ge(S["dtp"], then("dtp"))
                        for j in range(NH):
                            nc.scalar.activation(sp_a[:, j], pb[:, j * T:(j + 1) * T], ACT.Abs, bias=b_dt[:, j:j + 1])
                        for j in range(NH):
                            last = nc.scalar.activation(sp_r[:, j], pb[:, j * T:(j + 1) * T], ACT.Relu, bias=b_dt[:, j:j + 1])
                        last.then_inc(S["softp_a"], 1)
                    if query:
                        act.wait_ge(S["r1"], at_q("r1"))
                        nc.scalar.activation(qk_p[1][:], qk_r[:], ACT.Copy).then_inc(S["mid"], 1)
                    if prep:
                        act.wait_ge(S["softp_a"], then("softp_a"))
                        nc.scalar.activation(sp_a, sp_a, ACT.Exp, bias=zero[:], scale=-1.0).then_inc(S["softp_b"], 1)
                    if weigh:
                        keep_values(1)
                    if prep:
                        act.wait_ge(S["softp_b"], then("softp_b"))
                        nc.scalar.activation(sp_a, sp_a, ACT.Ln, bias=one[:]).then_inc(S["softp"], 1)
                    if scan:
                        keep_c(3, 0)
                    if query:
                        act.wait_ge(S["v"], at_q("v"))
                        nc.scalar.activation(vA[1 - p][:, :, :, 0:DK], qb[:, 0:NC * D].rearrange("p (c h k) -> p c h k", c=NC, k=DK),
                                             ACT.Copy).then_inc(S["vc"], 1)
                    if scan:
                        keep_c(3, 1)
                    if weigh:
                        inverse_sums(1)
                    if prep:
                        decay(2, 0)
                        decay(2, 1)
                    if weigh:
                        square(at_w, "mo", fb[0][:, 0:T], fsq)
                    if prep:
                        decay(3, 0)
                    if weigh:
                        inverse_root(at_w, link_f, "mo", fb[0][:, T:2 * T], eps_ln[:], frs)
                    if prep:
                        decay(3, 1)
                    if prep:
                        link_p.close()
                    if query:
                        link_q.close()
                    if weigh:
                        link_f.close()
                pipeline(act, turn)

            @block.vector
            def _(dve):
                tt, ts, stt = nc.vector.tensor_tensor, nc.vector.tensor_scalar, nc.vector.scalar_tensor_tensor
                Hv = [t[:].rearrange("p (j n) t -> p j n t", j=NH) for t in H]

                def turn(k, d, p, prep, scan, query, maxi, weigh):
                    now, then = counts(dve, k, d), counts(dve, k, d + 1)
                    at_q, at_m, at_w = counts(dve, k, d - 1), counts(dve, k, d - 2), counts(dve, k, d - 3)
                    link_p, link_q = chained(dve, then, "dve_p"), chained(dve, at_q, "dve_q")
                    placed = times(dve, k, 16 * 6) + (d - 2) * (16 * 6)
                    link_m, link_f = chained(dve, at_m, "dve_m"), chained(dve, at_w, "dve_f")

                    def normed(at, link, tag, centered, result, scale):
                        dve.wait_ge(S[f"{tag}_rs"], at(f"{tag}_rs"))
                        link(tt(result, centered, scale, ALU.mult))

                    def clamp(g):
                        mine, unit = (now, g + 2) if g + 2 < NU else (then, g + 2 - NU)
                        dve.wait_ge(S["dec"], mine("dec", 2 * unit + 2))
                        ts(dA[g % 2][:, :, 1:T], dA[g % 2][:, :, 1:T], FLOOR, None, ALU.max).then_inc(S["clamp"], 1)

                    def inputs(g, q):
                        if g >= 2:
                            dve.wait_ge(S["sum"], now("sum", g - 1))
                        elif query:
                            dve.wait_ge(S["sum"], at_q("sum", g + 3))
                        dve.wait_ge(S["u"], now("u"))
                        dve.wait_ge(S["Bb"], now("Bb", 2 * g + q + 1))
                        r = ring[q][:].rearrange("p (n t) -> p n t", t=T)
                        for j in range(NH):
                            last = tt(Hv[g % 2][:, j, 2 * q:2 * q + 2], u_s[p][:, j:j + 1].to_broadcast([P, 2, T]), r, ALU.mult)
                        last.then_inc(S["Bused"], 1)

                    def scan_states(g):
                        dve.wait_ge(S["Bused"], now("Bused", 2 * g + 2))
                        dve.wait_ge(S["clamp"], now("clamp", g + 1))
                        flat = H[g % 2][:].rearrange("p z t -> p (z t)")
                        nc.vector.tensor_tensor_scan(flat, dA[g % 2][:].rearrange("p z t -> p (z t)"), flat, 0.0,
                                                     ALU.mult, ALU.add).then_inc(S["scan"], 1)

                    def divide(n):
                        dve.wait_ge(S["inv"], at_w("inv", n + 1))
                        tt(o_s[:, 2 * n:2 * n + 2], o_s[:, 2 * n:2 * n + 2], fb[n][:].rearrange("p (g t) -> p g t", t=T),
                           ALU.mult).then_inc(S["div"], 1)

                    def maxima(first, last):
                        for f in range(first, last):
                            c, e, h = f // 8, f % 2, f // 2 % 4 * 2
                            dve.wait_ge(S["smax"], at_m("smax", f + 1))
                            nc.vector.tensor_reduce(mx[:, c, e * HS + h:e * HS + h + 2], s0[:].rearrange("p (g m) -> p g m", m=T),
                                                    AX.X, ALU.max).then_inc(S["mx"], 1)

                    if isinstance(k, int) and k == 2:
                        dve.wait_ge(s_late, LATE)
                    if query:
                        if maxi:
                            dve.wait_ge(S["lo"], at_m("lo"))
                        dve.wait_ge(S["sum"], at_q("sum", NU))
                        for j in range(NH):
                            last = stt(y_s[:, j], sil[1 - p][:, j], skip[:, j:j + 1], y_sum[:, j], ALU.mult, ALU.add)
                        last.then_inc(S["yraw"], 1)
                    if prep:
                        link_p(nc.vector.tensor_copy(mod_p[:], column(mods, 0, 2, k, d + 1)))
                    if query:
                        link_q(nc.vector.tensor_copy(mod_q[:], column(mods, 2, 3, k, d - 1)))
                    if scan:
                        inputs(0, 0)
                    if maxi:
                        maxima(0, 1)
                    if scan:
                        inputs(0, 1)
                    if prep:
                        normed(then, link_p, "ln1", pb[:, 0:T], pcen[:], prs[:])
                        ts(h1[:], pcen[:], mod_p[:, 1:2], mod_p[:, 0:1], ALU.mult, ALU.add).then_inc(S["h1"], 1)
                    if scan:
                        scan_states(0)
                    if query:
                        dve.wait_ge(S["rms_rs"], at_q("rms_rs"))
                        for j in range(NH):
                            last = stt(y_s[:, j], y_s[:, j], rms_w[:, j:j + 1], qrs[:], ALU.mult, ALU.mult)
                        last.then_inc(S["yout"], 1)
                    if maxi:
                        maxima(1, 2)
                    if scan:
                        inputs(1, 0)
                        inputs(1, 1)
                    if query:
                        dve.wait_ge(S["mix"], at_q("mix"))
                        stt(token_block(x_all, k, d - 1), qb[:, 0:T], mod_q[:, 0:1], token_block(x_all, k, d - 1), ALU.mult, ALU.add).then_inc(S["x1"], 1)
                    if prep:
                        dve.wait_ge(S["tap0"], then("tap0"))
                        for tap in range(1, TAPS):
                            for j in range(NH):
                                ins = stt(pz[:, j], xp[:, j, tap:tap + T], w_conv[:, j, tap:tap + 1], pz[:, j], ALU.mult, ALU.add)
                            link_p(ins)
                    if scan:
                        scan_states(1)
                    if prep:
                        dve.wait_ge(S["z"], then("z"))
                        ts(pm[:], pz[:], LEAST, None, ALU.max).then_inc(S["cut"], 1)
                    if maxi:
                        maxima(2, 3)
                    if scan:
                        inputs(2, 0)
                        clamp(0)
                    if maxi:
                        maxima(3, 4)
                    if query:
                        normed(at_q, link_q, "ln2", qb[:, 0:T], qcen[:], qrs[:])
                        ts(token_block(xf_all, k, d - 1), qcen[:], mod_q[:, 2:3], mod_q[:, 1:2], ALU.mult, ALU.add).then_inc(S["h2"], 1)
                    if scan:
                        inputs(2, 1)
                    if maxi:
                        maxima(4, 5)
                    if scan:
                        scan_states(2)
                    if maxi:
                        maxima(5, 7)
                    if query:
                        normed(at_q, link_q, "at", qb[:, 0:T], qcen[:], qrs[:])
                        ts(hn[:], qcen[:], ln[:, 0:1], ln[:, 1:2], ALU.mult, ALU.add).then_inc(S["hn"], 1)
                    if maxi:
                        maxima(7, 8)
                    if scan:
                        clamp(1)
                    if maxi:
                        maxima(8, 9)
                    if prep:
                        to = bc[1 - p]
                        dve.wait_ge(S["rank"], then("rank"))
                        link_p(nc.vector.tensor_copy(to[:], pb[0:96, 0:T]))
                        link_p(tt(bc_v[0:64], pb[0:64, 0:T], to[0:64], ALU.subtract))
                        link_p(nc.vector.tensor_copy(to[0:64], bc_v[0:64]))
                        link_p(tt(bc_v[0:32], bc_v[0:32], to[0:32], ALU.subtract))
                        nc.vector.tensor_copy(to[0:32], bc_v[0:32]).then_inc(S["bc"], 1)
                    if maxi:
                        maxima(9, 10)
                    if scan:
                        inputs(3, 0)
                    if maxi:
                        maxima(10, 11)
                    if scan:
                        inputs(3, 1)
                    if query:
                        dve.wait_ge(S["hi"], at_q("hi"))
                        tt(qk_r[:], qb[:].rearrange("p (a t) -> p a t", t=T), qk_p[0][:], ALU.subtract).then_inc(S["r1"], 1)
                    if scan:
                        scan_states(3)
                    if query:
                        dve.wait_ge(S["mid"], at_q("mid"))
                        tt(qk_p[2][:], qk_r[:], qk_p[1][:], ALU.subtract).then_inc(S["lo"], 1)
                    if maxi:
                        maxima(11, 12)
                    if prep:
                        dve.wait_ge(S["softp"], then("softp"))
                        stt(dt_s[1 - p][:], sp_a, 1e-4, sp_r, ALU.add, ALU.add).then_inc(S["dt"], 1)
                    if maxi:
                        maxima(12, 13)
                    if weigh:
                        divide(0)
                    if maxi:
                        maxima(13, 14)
                    if weigh:
                        divide(1)
                    if maxi:
                        maxima(14, 15)
                    if weigh:
                        dve.wait_ge(S["proj"], at_w("proj"))
                        tt(x2, token_block(xf_all, k, d - 3), fb[0][:, 0:T], ALU.add).then_inc(S["x2"], 1)
                        link_f(nc.vector.tensor_copy(gb_f[:], column(mods, 5, 1, k, d - 3)))
                    if maxi:
                        maxima(15, 16)
                    if prep:
                        clamp(2)
                    if maxi:
                        if weigh:
                            dve.wait_ge(s_mrow, placed)
                        dve.wait_ge(S["mxT"], at_m("mxT"))
                        link_m(nc.vector.tensor_copy(mx_p[:, 0], s0[0:NHD, 0:T]))
                        link_m(tt(mx_r[:], s0[0:NHD, 0:T], mx_p[:, 0], ALU.subtract))
                        link_m(nc.vector.tensor_copy(mx_p[:, 1], mx_r[:]))
                        tt(mx_p[:, 2], mx_r[:], mx_p[:, 1], ALU.subtract).then_inc(S["mxp"], 1)
                    if weigh:
                        normed(at_w, link_f, "mo", fb[0][:, 0:T], fcen, frs)
                        ts(xf[:], fcen, ln[:, 2:3], ln[:, 3:4], ALU.mult, ALU.add).then_inc(S["xf"], 1)
                        stt(token_block(x_all, k, d - 3), x2, gb_f[:], token_block(x_all, k, d - 3), ALU.mult, ALU.add).then_inc(S["fin"], 1)
                    if prep:
                        clamp(3)
                    if weigh:
                        dve.wait_ge(S["tok"], at_w("tok"))
                        ts(token_block(xf_all, k, d - 3), fb[0][:, 0:T], 1.0, None, ALU.mult)
                        ts(token_block(lg_all, k, d - 3), fb[0][:, T:T + NC * E], 1.0, None, ALU.mult).then_inc(S["tokc"], 1)
                    if prep:
                        link_p.close()
                    if query:
                        link_q.close()
                    if maxi:
                        link_m.close()
                    if weigh:
                        link_f.close()
                pipeline(dve, turn)

            @block.tensor
            def _(pe):
                mm = nc.tensor.matmul

                def turn(k, d, p, prep, scan, query, maxi, weigh):
                    now, then = counts(pe, k, d), counts(pe, k, d + 1)
                    at_q, at_m, at_w = counts(pe, k, d - 1), counts(pe, k, d - 2), counts(pe, k, d - 3)
                    stacked = times(pe, k, 16 * 24) + (d - 1) * (16 * 24)
                    placed = times(pe, k, 16 * 6) + (d - 2) * (16 * 6)

                    def center(tag, source, to):
                        mm(to[:, 0:T], center_d[:], source, start=True, stop=True).then_inc(S[f"{tag}_cen"], 1)

                    def variance(at, tag, source, to, over=mean_d, squares=None):
                        squares = squares or f"{tag}_sq"
                        pe.wait_ge(S[squares], at(squares))
                        mm(to[:, T:2 * T], over[:], source, start=True, stop=True).then_inc(S[f"{tag}_var"], 1)

                    def broadcast(name, g, q, first):
                        for n in range(2):
                            row = pick[:, first + g * U + 2 * q + n:first + g * U + 2 * q + n + 1]
                            last = mm(ring[q][:, n * T:(n + 1) * T], row.to_broadcast([96, P]), bc[p][:], start=True, stop=True)
                        last.then_inc(S[name], 1)

                    def broadcast_b(g, q):
                        if g:
                            pe.wait_ge(S["Cc"], now("Cc", 2 * g - 1 + q))
                        elif query:
                            pe.wait_ge(S["Cc"], at_q("Cc", 2 * NU - 1 + q))
                        pe.wait_ge(S["bc"], now("bc"))
                        broadcast("Bb", g, q, 0)

                    def broadcast_c(g, q):
                        pe.wait_ge(S["Bused"], now("Bused", 2 * g + q + 1))
                        broadcast("Cb", g, q, NS)

                    def scores(first, last):
                        for f in range(first, last):
                            c, e, h = f // 8, f % 2, f // 2 % 4 * 2
                            if f == 0:
                                if weigh:
                                    pe.wait_ge(S["mxp"], at_w("mxp"))
                                pe.wait_ge(s_stack, stacked)
                            if f >= 1:
                                pe.wait_ge(S["mx"], at_m("mx", f))
                            rows = slice(64 * e, 64 * e + KR)
                            for n in range(2):
                                ins = mm(s0[:, n * T:(n + 1) * T], stack[p][rows, 0, h + n, c * P:(c + 1) * P],
                                         stack[p][rows, 1, h + n, :], start=True, stop=True)
                            ins.then_inc(S["smax"], 1)

                    def head_scores(h):
                        e, n = h % 2, h // 2
                        if h == 0:
                            pe.wait_ge(s_mrow, placed)
                        else:
                            pe.wait_ge(S["pt"], at_w("pt", h))
                        rows = slice(64 * e, 64 * e + KR + 3)
                        for c in range(NC):
                            ins = mm(wb[:, c * T:(c + 1) * T], stack[1 - p][rows, 1, n, c * P:(c + 1) * P],
                                     stack[1 - p][rows, 0, n, :], start=True, stop=True)
                        ins.then_inc(S["st"], 1)

                    def values(h):
                        if h == 0:
                            pe.wait_ge(S["tokc"], at_w("tokc", 0))
                        pe.wait_ge(S["pt"], at_w("pt", h + 1))
                        g, rows = h // HPG, slice(VR * (h % HPG), VR * (h % HPG + 1))
                        for m in range(NC):
                            last = mm(fb[g // 2][rows, g % 2 * T:(g % 2 + 1) * T], vA[1 - p][:, m, h], PT[:, h % RD, m], start=m == 0, stop=m == NC - 1)
                        if h % (NHD // 2) == NHD // 2 - 1:
                            last.then_inc(S["pv"], 1)

                    def denominators(n):
                        pe.wait_ge(S["vs"], at_w("vs", n + 1))
                        for g in range(2):
                            last = mm(fb[n][:, g * T:(g + 1) * T], spread[:], o_s[:, 2 * n + g], start=True, stop=True)
                        last.then_inc(S["den"], 1)

                    if scan:
                        broadcast_b(0, 0)
                    if prep:
                        if scan:
                            pe.wait_ge(S["softp_a"], now("softp_a"))
                        center("ln1", token_block(x_all, k, d + 1), pb)
                    if scan:
                        broadcast_b(0, 1)
                    if maxi:
                        scores(0, 1)
                    if prep:
                        variance(then, "ln1", psq[:], pb)
                    if scan:
                        broadcast_c(0, 0)
                    if maxi:
                        scores(1, 2)
                    if scan:
                        broadcast_b(1, 0)
                    if query:
                        if maxi:
                            pe.wait_ge(S["vc"], at_m("vc"))
                        variance(at_q, "rms", qsq[:, 0], qb, mean_i, "rms_add")
                    if scan:
                        broadcast_c(0, 1)
                    if prep:
                        pe.wait_ge(S["h1"], then("h1"))
                        for j in range(NH):
                            last = mm(pb[:, j * T:(j + 1) * T], w_inT[:, j * P:(j + 1) * P], h1[:], start=True, stop=True)
                        last.then_inc(S["xz_x"], 1)
                    if weigh:
                        head_scores(0)
                    if scan:
                        broadcast_b(1, 1)
                    if prep:
                        pe.wait_ge(S["xp"], then("xp"))
                        for j in range(NH):
                            last = mm(pb[:, j * T:(j + 1) * T], w_inT[:, (NH + j) * P:(NH + j + 1) * P], h1[:], start=True, stop=True)
                        last.then_inc(S["xz_z"], 1)
                    if weigh:
                        head_scores(1)
                        values(0)
                    if query:
                        pe.wait_ge(S["yout"], at_q("yout"))
                        for j in range(NH):
                            last = mm(qb[:, 0:T], w_outT[:, j], y_s[:, j], start=j == 0, stop=j == NH - 1)
                        last.then_inc(S["mix"], 1)
                    if maxi:
                        scores(2, 3)
                    if weigh:
                        head_scores(2)
                        values(1)
                    if scan:
                        broadcast_c(1, 0)
                    if weigh:
                        head_scores(3)
                        values(2)
                    if query:
                        pe.wait_ge(S["x1"], at_q("x1"))
                        center("ln2", token_block(x_all, k, d - 1), qb)
                    if scan:
                        broadcast_c(1, 1)
                    if weigh:
                        head_scores(4)
                        values(3)
                    if scan:
                        broadcast_b(2, 0)
                    if weigh:
                        head_scores(5)
                        values(4)
                    if query:
                        variance(at_q, "ln2", qsq[:, 0], qb)
                    if weigh:
                        head_scores(6)
                        values(5)
                    if maxi:
                        scores(3, 4)
                    if scan:
                        broadcast_b(2, 1)
                    if weigh:
                        head_scores(7)
                        values(6)
                    if scan:
                        broadcast_c(2, 0)
                    if weigh:
                        head_scores(8)
                        values(7)
                    if maxi:
                        scores(4, 5)
                    if query:
                        pe.wait_ge(S["h2"], at_q("h2"))
                        center("at", token_block(xf_all, k, d - 1), qb)
                    if weigh:
                        head_scores(9)
                        values(8)
                    if maxi:
                        scores(5, 6)
                    if query:
                        variance(at_q, "at", qsq[:, 1], qb)
                    if weigh:
                        values(9)
                        head_scores(10)
                    if scan:
                        broadcast_c(2, 1)
                    if maxi:
                        scores(6, 7)
                    if weigh:
                        head_scores(11)
                        values(10)
                    if maxi:
                        scores(7, 8)
                    if prep:
                        pe.wait_ge(S["silu"], then("silu"))
                        for j in range(NH):
                            last = mm(pb[0:96 + R, 0:T], w_dbl[:, j], sil[1 - p][:, j], start=j == 0, stop=j == NH - 1)
                        last.then_inc(S["dbl"], 1)
                    if weigh:
                        head_scores(12)
                        values(11)
                    if maxi:
                        scores(8, 9)
                    if weigh:
                        head_scores(13)
                        values(12)
                    if scan:
                        broadcast_b(3, 0)
                    if maxi:
                        scores(9, 10)
                    if weigh:
                        head_scores(14)
                        values(13)
                    if scan:
                        broadcast_b(3, 1)
                    if weigh:
                        denominators(0)
                        head_scores(15)
                    if maxi:
                        scores(10, 11)
                    if query:
                        pe.wait_ge(S["hn"], at_q("hn"))
                        for n, w in enumerate((w_q, w_k)):
                            last = mm(qb[:, n * T:(n + 1) * T], w[:], hn[:], start=True, stop=True)
                        last.then_inc(S["qk"], 1)
                    if prep:
                        pe.wait_ge(S["bc"], then("bc"))
                        for j in range(NH):
                            last = mm(pb[:, j * T:(j + 1) * T], w_dtT[96:96 + R, j * P:(j + 1) * P], rank_s[96:96 + R], start=True, stop=True)
                        last.then_inc(S["dtp"], 1)
                    if maxi:
                        scores(11, 12)
                    if scan:
                        broadcast_c(3, 0)
                    if weigh:
                        values(14)
                    if scan:
                        broadcast_c(3, 1)
                    if weigh:
                        values(15)
                    if query:
                        pe.wait_ge(S["r1"], at_q("r1"))
                        for c in range(NC):
                            last = mm(qb[:, c * D:(c + 1) * D], hn[:, c * P:(c + 1) * P], w_v[:], start=True, stop=True)
                        last.then_inc(S["v"], 1)
                    if weigh:
                        denominators(1)
                    if maxi:
                        scores(12, 15)
                    if weigh:
                        pe.wait_ge(S["div"], at_w("div", 2))
                        for g in range(HG):
                            last = mm(fb[0][:, 0:T], w_proj[:, g], o_s[:, g], start=g == 0, stop=g == HG - 1)
                        last.then_inc(S["proj"], 1)
                    if maxi:
                        scores(15, 16)
                    if weigh:
                        pe.wait_ge(S["x2"], at_w("x2"))
                        center("mo", x2, fb[0])
                    if maxi:
                        pe.wait_ge(S["mx"], at_m("mx", FILLS))
                        for c in range(NC):
                            last = nc.tensor.transpose(s0[0:NHD, c * P:(c + 1) * P], mx[:, c], ident[:])
                        last.then_inc(S["mxT"], 1)
                    if weigh:
                        variance(at_w, "mo", fsq, fb[0])
                        pe.wait_ge(S["xf"], at_w("xf"))
                        for c in range(NC):
                            nc.tensor.transpose(fb[0][:, c * P:(c + 1) * P], xf[:, c * P:(c + 1) * P], ident[:])
                        for c in range(NC):
                            mm(fb[0][:, T + c * E:T + (c + 1) * E], xf[:, c * P:(c + 1) * P], gate_w[:], start=True, stop=False)
                            last = mm(fb[0][:, T + c * E:T + (c + 1) * E], ones_row[:], gate_b[:], start=False, stop=True)
                        last.then_inc(S["tok"], 1)
                pipeline(pe, turn)

        logits = lg_all[:].rearrange("p b (c e) -> p (b c) e", e=E)
        by_expert = "p (e c) -> p e c"

        def flat(tile):
            return tile[:].rearrange("p z t -> p (z t)")

        def carve(tile, k):
            return flat(tile)[:, k * C * E:(k + 1) * C * E]
        is_top, key_r, tmp = [carve(H[0], k).rearrange("p (c e) -> p c e", e=E) for k in range(3)]
        total, inclusive, cmp, restart = [carve(H[1], k).rearrange(by_expert, e=E) for k in range(4)]
        top_l, top_k, pos_f, steps = [carve(H[0], 4)[:, k * C:(k + 1) * C] for k in range(4)]
        tiles_e, tiles_in, base_e, ones_e = [carve(H[0], 5)[:, k * E:(k + 1) * E] for k in range(4)]
        tile_no = carve(H[0], 6)[:, 0:NT]
        of_tile = flat(dA[0])[:, 0:NT * E].rearrange("p (n e) -> p n e", e=E)
        expert_f = flat(dA[1])[:, 0:NT]

        def along(t, shape):
            return t.rearrange("p (n a) -> p n a", a=1).to_broadcast(shape)

        def across(t, shape):
            return t.rearrange("p (a n) -> p a n", a=1).to_broadcast(shape)

        s_place = ctx.enter_context(nc.semaphore("s_place"))
        s_pconst = ctx.enter_context(nc.semaphore("s_pconst"))
        s_count = ctx.enter_context(nc.semaphore("s_count"))
        s_hot = ctx.enter_context(nc.semaphore("s_hot"))
        s_pos = ctx.enter_context(nc.semaphore("s_pos"))
        s_sort = ctx.enter_context(nc.semaphore("s_sort"))

        with nc.Block() as block:
            @block.gpsimd
            def _(pool):
                nc.gpsimd.memset(ones_b[:], 1.0)
                nc.gpsimd.memset(before[:], 1.0)
                nc.gpsimd.memset(restart, 1.0)
                nc.gpsimd.memset(ones_e, 1.0)
                nc.gpsimd.iota(steps, pattern=[[P, C]], base=0, channel_multiplier=0, allow_small_or_imprecise_dtypes=True)
                nc.gpsimd.iota(tile_no, pattern=[[1, NT]], base=0, channel_multiplier=0,
                               allow_small_or_imprecise_dtypes=True).then_inc(s_pconst, 1)
                pool.wait_ge(s_pconst, 1)
                nc.gpsimd.memset(restart[:, :, 0:1], 0.0)
                nc.gpsimd.affine_select(out=before[:], in_=before[:], compare_op=ALU.is_gt, fill=0.0, base=0,
                                        pattern=[[1, P]], channel_multiplier=-1).then_inc(s_pconst, 1)
                pool.wait_ge(s_late, LATE)
                pool.wait_ge(s_pos, 1)
                rows = xf_all[:].rearrange("p b t -> p (b t)")
                for c in range(C):
                    nc.gpsimd.indirect_dma_start(sorted_x, bass.IndirectOffsetOnAxis(ap=place[:, c:c + 1], axis=0),
                                                 rows[:, c * D:(c + 1) * D], None).then_inc(s_sort, 16)
                pool.wait_ge(s_sort, 16 * C)

            @block.vector
            def _(dve):
                tt, ts, stt = nc.vector.tensor_tensor, nc.vector.tensor_scalar, nc.vector.scalar_tensor_tensor
                count = 0

                def link(ins):
                    nonlocal count
                    count += 1
                    ins.then_inc(s_place, 1)
                    dve.wait_ge(s_place, count)

                link(nc.vector.tensor_reduce(top_l, logits, AX.X, ALU.max))
                link(tt(is_top, logits, along(top_l, [P, C, E]), ALU.is_equal))
                link(tt(key_r, is_top, across(rank_e[:], [P, C, E]), ALU.mult))
                link(nc.vector.tensor_reduce(top_k, key_r, AX.X, ALU.max))
                link(tt(is_top, key_r, along(top_k, [P, C, E]), ALU.is_equal))
                nc.vector.tensor_copy(hot_b[:], is_top).then_inc(s_hot, 1)
                dve.wait_ge(s_pconst, 2)
                dve.wait_ge(s_count, 1)
                link(nc.vector.tensor_copy(total, pb[:, 0:C * E].rearrange("p (c e) -> p e c", e=E)))
                link(nc.vector.tensor_tensor_scan(inclusive.rearrange("p e c -> p (e c)"), restart.rearrange("p e c -> p (e c)"),
                                                  total.rearrange("p e c -> p (e c)"), 0.0, ALU.mult, ALU.add))
                link(tt(cmp, inclusive[:, :, C - 1:C].to_broadcast([P, E, C]), across(steps, [P, E, C]), ALU.is_gt))
                link(nc.vector.tensor_reduce(tiles_e, cmp, AX.X, ALU.add))
                link(nc.vector.tensor_tensor_scan(tiles_in, ones_e, tiles_e, 0.0, ALU.mult, ALU.add))
                link(tt(base_e, tiles_in, tiles_e, ALU.subtract))
                link(tt(inclusive, inclusive, total, ALU.subtract))
                link(stt(inclusive, along(base_e, [P, E, C]), float(P), inclusive, ALU.mult, ALU.add))
                link(tt(tmp, inclusive.rearrange("p e c -> p c e"), qb[:, 0:C * E].rearrange("p (c e) -> p c e", e=E), ALU.add))
                link(tt(tmp, tmp, is_top, ALU.mult))
                link(nc.vector.tensor_reduce(pos_f, tmp, AX.X, ALU.add))
                nc.vector.tensor_copy(place[:], pos_f).then_inc(s_pos, 1)
                link(tt(of_tile, across(tiles_in, [P, NT, E]), along(tile_no, [P, NT, E]), ALU.is_le))
                link(nc.vector.tensor_reduce(expert_f, of_tile, AX.X, ALU.add))
                link(ts(expert_f, expert_f, float(E - 1), None, ALU.min))
                link(nc.vector.tensor_copy(expert_i[:], expert_f))

            @block.tensor
            def _(pe):
                pe.wait_ge(s_pconst, 2)
                pe.wait_ge(s_hot, 1)
                nc.tensor.matmul(pb[:, 0:C * E], ones_b[:], hot_b[:], start=True, stop=True)
                nc.tensor.matmul(qb[:, 0:C * E], before[:], hot_b[:], start=True, stop=True).then_inc(s_count, 1)

        x_in = [flat(dA[0])[:, k * D:(k + 1) * D] for k in range(2)]
        x_t = [flat(dA[0])[:, (2 + k) * D:(3 + k) * D] for k in range(2)]
        y_o = [flat(dA[0])[:, (4 + k) * D:(5 + k) * D] for k in range(2)]
        hid = [flat(H[0])[:, k * HC * P:(k + 1) * HC * P] for k in range(2)]
        hid_t = [flat(H[1])[:, k * HC * P:(k + 1) * HC * P] for k in range(2)]
        up_bank, turn_bank, y_bank = [ring0, ring1], [s0, wb], [qb, f0]
        s_in = [ctx.enter_context(nc.semaphore(f"s_in{k}")) for k in range(2)]
        s_out = [ctx.enter_context(nc.semaphore(f"s_out{k}")) for k in range(2)]

        def over_tiles(eng, turn):
            def peeled(i):
                turn(i, i % 2, i + 1 < NT, 0 <= i < NT, 0 <= i - 1 < NT, 0 <= i - 2 < NT, i == NT - 1)
            for i in range(-1, 3):
                peeled(i)
            with eng.Fori(3, NT - 4, 4) as i:
                for n in range(4):
                    turn(i + n, (1 + n) % 2, True, True, True, True, n == 0)
            for i in range(NT - 1, NT + 2):
                peeled(i)

        def rows_of(t, i):
            return t[bass.ds(i * P, P), :]

        with nc.Block() as block:
            @block.sync
            def _(sp):
                def turn(i, q, ahead, up, down, store, fresh):
                    at, before_last = counts(sp, i), counts(sp, i, -2)
                    if ahead:
                        if up and down:
                            sp.wait_ge(S["e_turned"], at("e_turned", 0))
                        sp.dma_start(x_in[1 - q], rows_of(sorted_x, i + 1)).then_inc(s_in[1 - q], 16)
                    if store:
                        sp.wait_ge(S["e_y"], before_last("e_y"))
                        sp.dma_start(rows_of(sorted_y, i - 2), y_o[q]).then_inc(s_out[q], 16)
                for k in range(2):
                    sp.sem_inc(s_out[k], 16)
                over_tiles(sp, turn)
                for k in range(2):
                    sp.wait_ge(s_out[k], 16 * (NT // 2) + 16)

            @block.scalar
            def _(act):
                def turn(i, q, ahead, up, down, store, fresh):
                    at, last = counts(act, i), counts(act, i, -1)
                    stored = (i + q) * 8
                    if not isinstance(i, int):
                        stored = act.snap(stored)
                    if up:
                        act.wait_ge(S["e_up"], at("e_up"))
                        nc.scalar.activation(hid[q], up_bank[q][:], ACT.Gelu_apprx_tanh, bias=zero[:]).then_inc(S["e_gelu"], 1)
                    if down:
                        act.wait_ge(s_out[1 - q], stored)
                        act.wait_ge(S["e_down"], last("e_down"))
                        nc.scalar.activation(y_o[1 - q], y_bank[1 - q][:, 0:D], ACT.Copy).then_inc(S["e_y"], 1)
                over_tiles(act, turn)

            @block.vector
            def _(dve):
                def turn(i, q, ahead, up, down, store, fresh):
                    at, last = counts(dve, i, 1), counts(dve, i, -1)
                    if ahead:
                        dve.wait_ge(S["e_turned"], at("e_turned"))
                        nc.vector.tensor_copy(x_t[1 - q], pb[:, 0:P]).then_inc(S["e_xt"], 1)
                    if down:
                        dve.wait_ge(S["e_ht"], last("e_ht"))
                        nc.vector.tensor_copy(hid_t[1 - q], turn_bank[1 - q][:]).then_inc(S["e_htc"], 1)
                over_tiles(dve, turn)

            @block.tensor
            def _(pe):
                mm = nc.tensor.matmul
                e = e_last = None

                def turn(i, q, ahead, up, down, store, fresh):
                    nonlocal e, e_last
                    at, last = counts(pe, i), counts(pe, i, -1)
                    loaded = (i + 1 + q) * 8 + 8
                    if not isinstance(i, int):
                        loaded = pe.snap(loaded)
                    if down:
                        e_last = e
                        if fresh:
                            e_last = pe.value_load(expert_i[0:1, bass.ds(i - 1, 1)], min_val=0, max_val=E - 1)
                    if up:
                        e = pe.value_load(expert_i[0:1, bass.ds(i, 1)], min_val=0, max_val=E - 1)
                    if ahead:
                        if up:
                            pe.wait_ge(S["e_xt"], at("e_xt"))
                        pe.wait_ge(s_in[1 - q], loaded)
                        nc.tensor.transpose(pb[:, 0:P], x_in[1 - q], ident[:]).then_inc(S["e_turned"], 1)
                    if down:
                        pe.wait_ge(S["e_gelu"], last("e_gelu"))
                        for c in range(HC):
                            ins = nc.tensor.transpose(turn_bank[1 - q][:, c * P:(c + 1) * P], hid[1 - q][:, c * P:(c + 1) * P], ident[:])
                        ins.then_inc(S["e_ht"], 1)
                    if up:
                        pe.wait_ge(S["e_xt"], at("e_xt"))
                        mm(up_bank[q][:], x_t[q], w1[:, bass.ds(e, 1), :].rearrange("p a h -> p (a h)"), start=True, stop=True).then_inc(S["e_up"], 1)
                    if down:
                        pe.wait_ge(S["e_htc"], last("e_htc"))
                        for c in range(HC):
                            ins = mm(y_bank[1 - q][:, 0:D], hid_t[1 - q][:, c * P:(c + 1) * P], w2[:, bass.ds(e_last, 1), c, :].rearrange("p a d -> p (a d)"),
                                     start=c == 0, stop=c == HC - 1)
                        ins.then_inc(S["e_down"], 1)
                over_tiles(pe, turn)

        y_tok = [flat(dA[1])[:, k * NC * D:(k + 1) * NC * D] for k in range(2)]
        ot = [y_s[:, k] for k in range(2)]
        s_back = [ctx.enter_context(nc.semaphore(f"s_back{k}")) for k in range(2)]
        s_store = [ctx.enter_context(nc.semaphore(f"s_store{k}")) for k in range(2)]

        with nc.Block() as block:
            @block.sync
            def _(sp):
                for q in range(2):
                    sp.sem_inc(s_store[q], 16)
                with sp.Fori(0, B - 1, 2) as b:
                    for q in range(2):
                        at = counts(sp, b, q)
                        sp.wait_ge(S["f_out"], at("f_out"))
                        sp.dma_start(out[bass.ds(b + q, 1)].rearrange("a d t -> (a d) t"), ot[q]).then_inc(s_store[q], 16)
                for q in range(2):
                    sp.wait_ge(s_store[q], 16 * (B // 2) + 16)

            @block.gpsimd
            def _(pool):
                for b in range(B):
                    q, at = b % 2, counts(pool, b, -2)
                    if b >= 2:
                        pool.wait_ge(s_back[q], b // 2 * 32)
                    pool.wait_ge(S["f_turned"], at("f_turned"))
                    for c in range(NC):
                        nc.gpsimd.indirect_dma_start(y_tok[q][:, c * D:(c + 1) * D], None, sorted_y,
                                                     bass.IndirectOffsetOnAxis(ap=place[:, b * NC + c:b * NC + c + 1], axis=0)).then_inc(s_back[q], 16)

            @block.vector
            def _(dve):
                with dve.Fori(0, B - 1, 2) as b:
                    stored = dve.snap(b * 8 + 16)
                    for q in range(2):
                        at = counts(dve, b, q)
                        dve.wait_ge(S["f_out"], at("f_out", 0))
                        nc.vector.tensor_scalar(gb_f[:], column(mods, 5, 1, b, q), 1.0, None, ALU.mult).then_inc(S["f_gate"], 1)
                        dve.wait_ge(S["f_gate"], at("f_gate"))
                        dve.wait_ge(s_store[q], stored)
                        dve.wait_ge(S["f_turned"], at("f_turned"))
                        nc.vector.scalar_tensor_tensor(ot[q], ring[q][:, 0:T], gb_f[:], token_block(x_all, b, q), ALU.mult, ALU.add).then_inc(S["f_out"], 1)

            @block.tensor
            def _(pe):
                with pe.Fori(0, B - 1, 2) as b:
                    back = pe.snap(b * 16 + 32)
                    for q in range(2):
                        at = counts(pe, b, q - 2)
                        pe.wait_ge(S["f_out"], at("f_out"))
                        pe.wait_ge(s_back[q], back)
                        for c in range(NC):
                            last = nc.tensor.transpose(ring[q][:, c * P:(c + 1) * P], y_tok[q][:, c * D:(c + 1) * D], ident[:])
                        last.then_inc(S["f_turned"], 1)


def kernel(**inputs):
    import numpy as np
    import concourse.bacc as bacc
    from concourse import mybir as mb
    from concourse.bass_utils import run_bass_kernel_spmd as run

    a = {k: np.asarray(v) for k, v in inputs.items()}
    P, DK = 128, 8

    def halves(v):
        return v.reshape((2, P) + v.shape[1:]).swapaxes(0, 1)

    w_xT = a["L0_attn_W_x"].T
    rank = a["L0_attn_W_dt"].shape[1]
    bc_cols = w_xT[:, rank:]

    def tiled_heads(w):
        return w.reshape(w.shape[0], -1, 2, DK).transpose(0, 2, 3, 1).reshape(w.shape[0], -1)

    qkv = a["L0_ffn_w_qkv"]
    D = qkv.shape[0]
    data = {
        "x": a["L0_attn_x"].transpose(0, 2, 1),
        "w_inT": a["L0_attn_W_in"].T,
        "w_conv": halves(a["L0_attn_W_conv"]),
        "b_conv": halves(a["L0_attn_b_conv"]),
        "w_dbl": halves(np.concatenate([bc_cols, bc_cols, bc_cols, w_xT[:, :rank]], axis=1)),
        "w_dtT": a["L0_attn_W_dt"].T,
        "b_dt": halves(a["L0_attn_b_dt"]),
        "a_log": halves(a["L0_attn_A_log"]),
        "skip": halves(a["L0_attn_D"]),
        "rms_w": halves(a["L0_attn_rms_w"]),
        "w_outT": halves(a["L0_attn_W_out"].T),
        "ln": np.stack([a["L0_ffn_ln1_w"], a["L0_ffn_ln1_b"], a["L0_ffn_ln2_w"], a["L0_ffn_ln2_b"]], axis=1),
        "w_q": tiled_heads(qkv[:, :D]),
        "w_k": tiled_heads(qkv[:, D:2 * D]),
        "w_v": qkv[:, 2 * D:],
        "w_proj": a["L0_ffn_w_proj"],
        "gate_w": a["L0_ffn_gate_w"],
        "gate_b": a["L0_ffn_gate_b"][None],
        "w1": a["L0_ffn_w1"],
        "w2": a["L0_ffn_w2"],
        "cT": a["L0_c"].T,
        "w_mod": a["L0_wmod"].reshape(D, 6, D),
    }
    nc = bacc.Bacc("TRN2", target_bir_lowering=False, num_devices=1)
    arrays, io = {}, {}
    for name, v in data.items():
        v = np.ascontiguousarray(v)
        arrays[f"in_{name}"] = v
        io[name] = nc.dram_tensor(f"in_{name}", v.shape, mb.dt.from_np(v.dtype), kind="ExternalInput").ap()
    out = nc.dram_tensor("out_0", data["x"].shape, mb.dt.float32, kind="ExternalOutput").ap()
    adaln_block(nc, io, out)
    r = run(nc, [arrays], core_ids=[0])
    return np.ascontiguousarray(r.results[0]["out_0"].transpose(0, 2, 1))
```
